# Optimizing a Trainium2 kernel written in Bass

```python
import numpy as np
import jax
import jax.numpy as jnp

def _softmax(x, axis=-1):
    return jax.nn.softmax(x, axis=axis)

def _gelu(x):
    return jax.nn.gelu(x, approximate=True)

def _silu(x):
    return jax.nn.silu(x)

def _sigmoid(x):
    return jax.nn.sigmoid(x)

def _layernorm(x, axis=-1, eps=1e-05):
    m = jnp.mean(x, axis=axis, keepdims=True)
    v = jnp.var(x, axis=axis, keepdims=True)
    return (x - m) / jnp.sqrt(v + eps)

def _scatter_add(tgt, idx, src, axis=0):
    return tgt.at[idx].add(src)

def _segment_sum(src, seg, n):
    return jax.ops.segment_sum(src, seg, n)
kernel_name = 'mk_decoder_postln_d1_seqx_r8_1399c3'

def setup_inputs(seed: int=0):
    np.random.seed(seed)
    _w = jnp.asarray

    def _rec_inputs():
        import jax
        import jax.numpy as jnp
        _rk = jax.random.key(seed)
        x = -0.000125 + 0.9999 * jax.random.normal(jax.random.fold_in(_rk, 1), (4, 256, 256), jnp.float32)
        _lenS = 256 - jax.random.randint(jax.random.fold_in(_rk, 7), (4,), 0, max(1, 256 // 4) + 1, jnp.int32)
        _lenS2 = 256 - jax.random.randint(jax.random.fold_in(_rk, 8), (4,), 0, max(1, 256 // 4) + 1, jnp.int32)
        itok_BxS_13_99985 = jax.random.randint(jax.random.fold_in(_rk, 11), (4, 256), 13, 99986, jnp.int32)
        _ctx_2048P = jax.random.normal(jax.random.fold_in(_rk, 12), (4, 16, 256), jnp.float32)
        _ctx_2048c = jax.random.dirichlet(jax.random.fold_in(_rk, 512), 0.3 * jnp.ones((16,), jnp.float32), (4, 256))
        _ctx_2048t = jnp.einsum('bsk,bkd->bsd', _ctx_2048c, _ctx_2048P)
        _ctx_2048t = _ctx_2048t * jax.lax.rsqrt(jnp.mean(jnp.square(_ctx_2048t)) + 1e-12) * 0.953939
        ctx_2048 = 6.82029e-06 + 0.0200006 * (_ctx_2048t + 0.3 * jax.random.normal(jax.random.fold_in(_rk, 612), (4, 256, 256), jnp.float32))
        return (x, itok_BxS_13_99985, ctx_2048)
    x, itok_BxS_13_99985, ctx_2048 = _rec_inputs()

    def _L0_attn_setup():
        import jax, jax.numpy as jnp
        import numpy as np
        N_EMBD = 256
        Q_HEAD = 16
        KV_HEAD = 4
        HEAD_DIM = N_EMBD // Q_HEAD
        ROPE_BASE = 10000.0

        def _rope(Y, d_rope, base=ROPE_BASE):
            b, h, t, d = Y.shape
            mid = d_rope // 2
            Y1 = Y[:, :mid]
            Y2 = Y[:, mid:]
            Ym1 = jnp.concatenate([Y1, Y2], axis=1)
            Ym2 = jnp.concatenate([-Y2, Y1], axis=1)
            inv = base ** (-2.0 * jnp.arange(d // 2, dtype=jnp.float32) / d)
            theta = jnp.arange(t, dtype=jnp.float32)[:, None] * inv[None, :]
            cos2 = jnp.concatenate([jnp.cos(theta), jnp.cos(theta)], axis=1)
            sin2 = jnp.concatenate([jnp.sin(theta), jnp.sin(theta)], axis=1)
            return Ym1 * cos2 + Ym2 * sin2

        def _attention(x, Wq, bq, Wk, bk, Wv, bv, Wo, bo):
            b, t, n = x.shape
            hd = n // Q_HEAD
            q = x @ Wq.T + bq
            k = x @ Wk.T + bk
            v = x @ Wv.T + bv
            q = q.reshape(b, t, Q_HEAD, hd).transpose(0, 2, 1, 3)
            k = k.reshape(b, t, KV_HEAD, hd).transpose(0, 2, 1, 3)
            v = v.reshape(b, t, KV_HEAD, hd).transpose(0, 2, 1, 3)
            q = _rope(q, N_EMBD)
            k = _rope(k, N_EMBD)
            rep = Q_HEAD // KV_HEAD
            k = jnp.repeat(k, rep, axis=1)
            v = jnp.repeat(v, rep, axis=1)
            scale = jnp.sqrt(jnp.float32(hd))
            att = jnp.einsum('bhqd,bhkd->bhqk', q, k) / scale
            causal = jnp.tril(jnp.ones((t, t), dtype=bool))
            att = jnp.where(causal[None, None], att, -jnp.inf)
            att = jax.nn.softmax(att, axis=-1)
            y = jnp.einsum('bhqt,bhtd->bhqd', att, v)
            y = y.transpose(0, 2, 1, 3).reshape(b, t, n)
            return y @ Wo.T + bo
        key = jax.random.key(seed)
        ks = jax.random.split(key, 9)
        kv_dim = HEAD_DIM * KV_HEAD
        s = 1.0 / np.sqrt(N_EMBD)
        return {'x': jax.random.normal(ks[0], (4, 128, N_EMBD), jnp.float32), 'Wq': jax.random.normal(ks[1], (N_EMBD, N_EMBD), jnp.float32) * s, 'bq': jax.random.normal(ks[2], (N_EMBD,), jnp.float32) * 0.01, 'Wk': jax.random.normal(ks[3], (kv_dim, N_EMBD), jnp.float32) * s, 'bk': jax.random.normal(ks[4], (kv_dim,), jnp.float32) * 0.01, 'Wv': jax.random.normal(ks[5], (kv_dim, N_EMBD), jnp.float32) * s, 'bv': jax.random.normal(ks[6], (kv_dim,), jnp.float32) * 0.01, 'Wo': jax.random.normal(ks[7], (N_EMBD, N_EMBD), jnp.float32) * s, 'bo': jax.random.normal(ks[8], (N_EMBD,), jnp.float32) * 0.01}
    _L0_attn_all = _L0_attn_setup()
    _L0_attn_in = {k: v for k, v in _L0_attn_all.items() if k in ('Wq', 'bq', 'Wk', 'bk', 'Wv', 'bv', 'Wo', 'bo')}
    del _L0_attn_all

    def _L0_xattn_setup():
        import jax, jax.numpy as jnp
        import numpy as np
        B, S, D = (4, 512, 256)
        E = 4
        F = 1024 // E
        VOCAB = 12500
        key = jax.random.key(seed)
        k1, k2, k3, k4, k5 = jax.random.split(key, 5)
        hidden_states = jax.random.normal(k1, (B, S, D), dtype=jnp.float32)
        token_ids = jax.random.randint(k2, (B, S), 0, VOCAB, dtype=jnp.int64)
        Wg = jax.random.normal(k3, (E, F, D), dtype=jnp.float32) * 0.02
        Wu = jax.random.normal(k4, (E, F, D), dtype=jnp.float32) * 0.02
        Wd = jax.random.normal(k5, (E, D, F), dtype=jnp.float32) * 0.02
        return {'hidden_states': hidden_states, 'token_ids': token_ids, 'Wg': Wg, 'Wu': Wu, 'Wd': Wd}
    _L0_xattn_all = _L0_xattn_setup()
    _L0_xattn_in = {k: v for k, v in _L0_xattn_all.items() if k in ()}
    del _L0_xattn_all

    def _L0_ffn_setup():
        import jax, jax.numpy as jnp
        import numpy as np
        B_, S, D = (2, 256, 256)
        F_ = 1024
        R = 16
        H = 16
        HD = D // H
        MOD_SCALE = 0.1
        EPS = 1e-06

        def _rmsnorm(x, w):
            v = jnp.mean(x * x, axis=-1, keepdims=True)
            return x * jax.lax.rsqrt(v + EPS) * w

        def _attention(x, Wq, Wk, Wv, Wo):
            b, s, d = x.shape
            q = (x @ Wq.T).reshape(b, s, H, HD)
            k = (x @ Wk.T).reshape(b, s, H, HD)
            v = (x @ Wv.T).reshape(b, s, H, HD)
            scores = jnp.einsum('bqhd,bkhd->bhqk', q, k) / np.sqrt(HD).astype(np.float32)
            causal = jnp.tril(jnp.ones((s, s), bool))
            scores = jnp.where(causal, scores, jnp.finfo(scores.dtype).min)
            probs = jax.nn.softmax(scores, axis=-1)
            out = jnp.einsum('bhqk,bkhd->bqhd', probs, v).reshape(b, s, d)
            return out @ Wo.T
        key = jax.random.key(seed)
        ks = jax.random.split(key, 12)
        sd = 0.02
        return {'hidden_states': jax.random.normal(ks[0], (B_, S, D), jnp.float32), 'ln1_w': jnp.ones((D,), jnp.float32), 'ln2_w': jnp.ones((D,), jnp.float32), 'Wq': jax.random.normal(ks[1], (D, D), jnp.float32) * sd, 'Wk': jax.random.normal(ks[2], (D, D), jnp.float32) * sd, 'Wv': jax.random.normal(ks[3], (D, D), jnp.float32) * sd, 'Wo': jax.random.normal(ks[4], (D, D), jnp.float32) * sd, 'A': jax.random.normal(ks[5], (D, R), jnp.float32) * (0.01 / np.sqrt(D)), 'B': jax.random.normal(ks[6], (R, F_), jnp.float32) * (0.01 / np.sqrt(R)), 'W_in_base': jax.random.normal(ks[7], (F_, D), jnp.float32) * sd, 'W_up_base': jax.random.normal(ks[8], (F_, D), jnp.float32) * sd, 'W_down': jax.random.normal(ks[9], (D, F_), jnp.float32) * sd}
    _L0_ffn_all = _L0_ffn_setup()
    _L0_ffn_in = {k: v for k, v in _L0_ffn_all.items() if k in ('ln1_w', 'ln2_w', 'Wq', 'Wk', 'Wv', 'Wo', 'A', 'B', 'W_in_base', 'W_up_base', 'W_down')}
    del _L0_ffn_all
    return {'x': x, 'itok_BxS_13_99985': itok_BxS_13_99985, 'ctx_2048': ctx_2048, 'L0_attn_Wq': _L0_attn_in['Wq'], 'L0_attn_bq': _L0_attn_in['bq'], 'L0_attn_Wk': _L0_attn_in['Wk'], 'L0_attn_bk': _L0_attn_in['bk'], 'L0_attn_Wv': _L0_attn_in['Wv'], 'L0_attn_bv': _L0_attn_in['bv'], 'L0_attn_Wo': _L0_attn_in['Wo'], 'L0_attn_bo': _L0_attn_in['bo'], 'L0_ffn_ln1_w': _L0_ffn_in['ln1_w'], 'L0_ffn_ln2_w': _L0_ffn_in['ln2_w'], 'L0_ffn_Wq': _L0_ffn_in['Wq'], 'L0_ffn_Wk': _L0_ffn_in['Wk'], 'L0_ffn_Wv': _L0_ffn_in['Wv'], 'L0_ffn_Wo': _L0_ffn_in['Wo'], 'L0_ffn_A': _L0_ffn_in['A'], 'L0_ffn_B': _L0_ffn_in['B'], 'L0_ffn_W_in_base': _L0_ffn_in['W_in_base'], 'L0_ffn_W_up_base': _L0_ffn_in['W_up_base'], 'L0_ffn_W_down': _L0_ffn_in['W_down']}

def reference(x, itok_BxS_13_99985, ctx_2048, L0_attn_Wq, L0_attn_bq, L0_attn_Wk, L0_attn_bk, L0_attn_Wv, L0_attn_bv, L0_attn_Wo, L0_attn_bo, L0_ffn_ln1_w, L0_ffn_ln2_w, L0_ffn_Wq, L0_ffn_Wk, L0_ffn_Wv, L0_ffn_Wo, L0_ffn_A, L0_ffn_B, L0_ffn_W_in_base, L0_ffn_W_up_base, L0_ffn_W_down):
    import jax
    import jax.numpy as jnp

    def _L0_attn_ref(x, Wq, bq, Wk, bk, Wv, bv, Wo, bo):
        import jax, jax.numpy as jnp
        import numpy as np
        N_EMBD = 256
        Q_HEAD = 16
        KV_HEAD = 4
        HEAD_DIM = N_EMBD // Q_HEAD
        ROPE_BASE = 10000.0

        def _rope(Y, d_rope, base=ROPE_BASE):
            b, h, t, d = Y.shape
            mid = d_rope // 2
            Y1 = Y[:, :mid]
            Y2 = Y[:, mid:]
            Ym1 = jnp.concatenate([Y1, Y2], axis=1)
            Ym2 = jnp.concatenate([-Y2, Y1], axis=1)
            inv = base ** (-2.0 * jnp.arange(d // 2, dtype=jnp.float32) / d)
            theta = jnp.arange(t, dtype=jnp.float32)[:, None] * inv[None, :]
            cos2 = jnp.concatenate([jnp.cos(theta), jnp.cos(theta)], axis=1)
            sin2 = jnp.concatenate([jnp.sin(theta), jnp.sin(theta)], axis=1)
            return Ym1 * cos2 + Ym2 * sin2

        def _attention(x, Wq, bq, Wk, bk, Wv, bv, Wo, bo):
            b, t, n = x.shape
            hd = n // Q_HEAD
            q = x @ Wq.T + bq
            k = x @ Wk.T + bk
            v = x @ Wv.T + bv
            q = q.reshape(b, t, Q_HEAD, hd).transpose(0, 2, 1, 3)
            k = k.reshape(b, t, KV_HEAD, hd).transpose(0, 2, 1, 3)
            v = v.reshape(b, t, KV_HEAD, hd).transpose(0, 2, 1, 3)
            q = _rope(q, N_EMBD)
            k = _rope(k, N_EMBD)
            rep = Q_HEAD // KV_HEAD
            k = jnp.repeat(k, rep, axis=1)
            v = jnp.repeat(v, rep, axis=1)
            scale = jnp.sqrt(jnp.float32(hd))
            att = jnp.einsum('bhqd,bhkd->bhqk', q, k) / scale
            causal = jnp.tril(jnp.ones((t, t), dtype=bool))
            att = jnp.where(causal[None, None], att, -jnp.inf)
            att = jax.nn.softmax(att, axis=-1)
            y = jnp.einsum('bhqt,bhtd->bhqd', att, v)
            y = y.transpose(0, 2, 1, 3).reshape(b, t, n)
            return y @ Wo.T + bo
        return _attention(x, Wq, bq, Wk, bk, Wv, bv, Wo, bo)

    def _L0_xattn_ref(hidden_states, token_ids, Wg, Wu, Wd):
        import jax, jax.numpy as jnp
        import numpy as np
        B, S, D = (4, 512, 256)
        E = 4
        F = 1024 // E
        VOCAB = 12500
        tokens_per_expert = VOCAB // E
        tid = jnp.clip(token_ids, 0, VOCAB - 1)
        expert_ids = jnp.minimum(tid // tokens_per_expert, E - 1)
        out = jnp.zeros_like(hidden_states)
        for e in range(E):
            g = jax.nn.silu(jnp.einsum('bsd,fd->bsf', hidden_states, Wg[e]))
            u = jnp.einsum('bsd,fd->bsf', hidden_states, Wu[e])
            y = jnp.einsum('bsf,df->bsd', g * u, Wd[e])
            out = jnp.where((expert_ids == e)[..., None], y, out)
        return out

    def _L0_ffn_ref(hidden_states, ln1_w, ln2_w, Wq, Wk, Wv, Wo, A, B, W_in_base, W_up_base, W_down):
        import jax, jax.numpy as jnp
        import numpy as np
        B_, S, D = (2, 256, 256)
        F_ = 1024
        R = 16
        H = 16
        HD = D // H
        MOD_SCALE = 0.1
        EPS = 1e-06

        def _rmsnorm(x, w):
            v = jnp.mean(x * x, axis=-1, keepdims=True)
            return x * jax.lax.rsqrt(v + EPS) * w

        def _attention(x, Wq, Wk, Wv, Wo):
            b, s, d = x.shape
            q = (x @ Wq.T).reshape(b, s, H, HD)
            k = (x @ Wk.T).reshape(b, s, H, HD)
            v = (x @ Wv.T).reshape(b, s, H, HD)
            scores = jnp.einsum('bqhd,bkhd->bhqk', q, k) / np.sqrt(HD).astype(np.float32)
            causal = jnp.tril(jnp.ones((s, s), bool))
            scores = jnp.where(causal, scores, jnp.finfo(scores.dtype).min)
            probs = jax.nn.softmax(scores, axis=-1)
            out = jnp.einsum('bhqk,bkhd->bqhd', probs, v).reshape(b, s, d)
            return out @ Wo.T
        residual = hidden_states
        x = _rmsnorm(hidden_states, ln1_w)
        attn = _attention(x, Wq, Wk, Wv, Wo)
        mod = MOD_SCALE * jnp.tanh(attn @ A)
        h = _rmsnorm(residual, ln2_w)
        gate_pre = h @ W_in_base.T + mod * (h @ A) @ B
        gate = jax.nn.silu(gate_pre)
        up = h @ W_up_base.T
        mlp_out = gate * up @ W_down.T
        return residual + mlp_out
    x = _layernorm(x + _L0_attn_ref(x, L0_attn_Wq, L0_attn_bq, L0_attn_Wk, L0_attn_bk, L0_attn_Wv, L0_attn_bv, L0_attn_Wo, L0_attn_bo), axis=-1)
    x = _layernorm(x + _L0_xattn_ref(x, itok_BxS_13_99985, ctx_2048, ctx_2048, ctx_2048), axis=-1)
    x = _layernorm(x + _L0_ffn_ref(x, L0_ffn_ln1_w, L0_ffn_ln2_w, L0_ffn_Wq, L0_ffn_Wk, L0_ffn_Wv, L0_ffn_Wo, L0_ffn_A, L0_ffn_B, L0_ffn_W_in_base, L0_ffn_W_up_base, L0_ffn_W_down), axis=-1)
    return x

_drawn_inputs = setup_inputs


def setup_inputs(seed=0):
    import zlib

    import numpy as np

    out = dict(_drawn_inputs(seed))
    spreads = {'L0_ffn_ln1_w': (1.0, 0.6), 'L0_ffn_ln2_w': (1.0, 0.6)}
    factors = {'L0_attn_bq': 8.0,
     'L0_attn_bk': 25.137,
     'L0_attn_bv': 4.993,
     'L0_attn_bo': 6.064,
     'L0_ffn_Wq': 64.0,
     'L0_ffn_Wk': 64.0,
     'L0_ffn_Wv': 64.0,
     'L0_ffn_Wo': 64.0,
     'L0_ffn_A': 64.0,
     'L0_ffn_B': 64.0,
     'L0_ffn_W_in_base': 3.032,
     'L0_ffn_W_up_base': 2.989,
     'L0_ffn_W_down': 3.001}
    for name, (base, spread) in spreads.items():
        noise = np.random.default_rng([zlib.crc32(name.encode()), seed]).standard_normal(out[name].shape)
        drawn = base * np.exp(spread * noise) if base else spread * noise
        out[name] = jnp.asarray(drawn.astype(out[name].dtype))
    for name, factor in factors.items():
        out[name] = (out[name] * factor).astype(out[name].dtype)
    return out
```

```python
from contextlib import ExitStack

import numpy as np

import concourse.bass as bass
from concourse import mybir

P = 128
BATCHES, SEQ, D = 4, 256, 256
TOKENS = BATCHES * SEQ
TILES = TOKENS // P
HALF = 512
HALVES = TOKENS // HALF
HT = HALF // P
KT = D // P
HEADS, HD = 16, 16
KV_HEADS = 4
GROUP = 4
GROUPS = HEADS // GROUP
VW = 32
EXPERTS, EF = 4, 256
TOKENS_PER_EXPERT = 12500 // EXPERTS
FF = 1024
FT = FF // P
RANK = 16
MOD_SCALE = 0.1
LN_EPS, RMS_EPS = 1e-5, 1e-6
SM_SCALE = HD ** -0.5
MASKED = -1e30
TERMS = [(0, 0), (0, 1), (0, 2), (1, 0), (1, 1), (2, 0)]
STACK = HD * len(TERMS)
PARTS = 3
DMA_DONE = 16

F32, BF16, I32 = mybir.dt.float32, mybir.dt.bfloat16, mybir.dt.int32
ALU = mybir.AluOpType
ACT = mybir.ActivationFunctionType
AX = mybir.AxisListType.X
ONES_PAIR = float(np.array([0x3F803F80], np.uint32).view(np.float32)[0])

RING = {"PROJ": 1, "V": 1, "S": 1, "MAXT": 1, "ST": 1, "YT": 1, "WO": 1, "TR": 2, "HID": 1, "MOD": 1,
        "WOA": 1}


def make_plan():
    plan = []
    add = lambda *step: plan.append(step)

    def project(a, u):
        for w in "qk":
            add("PROJ", a, u, w)
            add("CAST", a, u, w)

    def maxima(a, b):
        for g in range(GROUPS):
            add("S", a, b, g)
        add("MAXT", a, b)

    def close_pair(a, b, pair):
        add("EVAC", a, b, pair)
        add("TURN", a, b, pair)

    def after(a, b):
        add("YT", a, b)
        if a == 0:
            add("WO", a, b)
            add("RSTD", "ln1", b)
            add("NORM", "ln1", b)
        else:
            add("MOD", a, b)

    def attend(a, batches, upcoming, extra=None):
        extra = extra or {}
        for i, b in enumerate(batches):
            nxt = batches[i + 1] if i + 1 < len(batches) else upcoming
            for g in range(GROUPS):
                if nxt is not None:
                    add("S", a, nxt, g)
                add("ST", a, b, g)
                if g:
                    add("PV", a, b, g - 1)
                elif i:
                    add("PV", a, batches[i - 1], GROUPS - 1)
                    add("EVAC", a, batches[i - 1], 1)
                if g == 1 and i:
                    add("TURN", a, batches[i - 1], 1)
                if g == 2 and i:
                    after(a, batches[i - 1])
                if g == 2:
                    add("EVAC", a, b, 0)
                if g == 3:
                    add("TURN", a, b, 0)
            if nxt is not None:
                add("MAXT", a, nxt)
            for step in extra.get(b, ()):
                step()
        last = batches[-1]
        add("PV", a, last, GROUPS - 1)
        close_pair(a, last, 1)
        after(a, last)

    def moe(u, middle=None, end=None):
        for e in range(EXPERTS):
            add("HID", "moe", u, e)
            if e:
                add("DOWN", "moe", u, e - 1)
            if e == 1 and middle:
                middle()
        if end:
            end()
        add("DOWN", "moe", u, EXPERTS - 1)
        for kind in ("ln2", "rms"):
            add("RSTD", kind, u)
            add("NORM", kind, u)

    def ffn(u, middle=None):
        for f in range(FT):
            add("HID", "ffn", u, f)
            if f:
                add("DOWN", "ffn", u, f - 1)
            if f == 2 and middle:
                middle()
        add("DOWN", "ffn", u, FT - 1)
        add("RSTD", "ln3", u)
        add("NORM", "ln3", u)
        add("OUT", u)

    for u in range(HALVES):
        project(0, u)
        add("V", 0, u)
    maxima(0, 0)
    add("WOA")
    attend(0, [0, 1, 2, 3], None)
    add("TR", "x1", 0)
    moe(0)
    add("TR", "x1", 1)

    def second_attention():
        add("TR", "xn", 0)
        project(1, 0)
        add("V", 1, 0)

    moe(1, middle=second_attention, end=lambda: maxima(1, 0))

    def second_half():
        add("TR", "xn", 1)
        project(1, 1)

    attend(1, [0, 1], None, extra={0: [second_half]})
    add("V", 1, 1)
    ffn(0, middle=lambda: maxima(1, 2))
    attend(1, [2, 3], None)
    ffn(1)
    return plan


PLAN = make_plan()


def count_steps():
    nth, ring, seen, filled, released = {}, {}, {}, [0, 0], [0, 0]
    for step in PLAN:
        kind = step[0]
        seen[kind] = seen.get(kind, 0) + 1
        nth[step] = seen[kind]
        if kind in RING:
            slot = sum(filled) % 2
            filled[slot] += 1
            ring[step] = (slot, filled[slot], released[slot])
            released[slot] += RING[kind]
    return nth, ring


NTH, RING_AT = count_steps()


def step_at(kind, n):
    return [s for s in PLAN if s[0] == kind][n - 1]


def decoder_layer(nc, x_tok, x_feat, token_ids, ctx_t, wq1, bq1, wk1, bk1, wv1, bv1, wo1, bo1, ln1, ln2,
                  wq2, wk2, wv2, wo2, a_in, b_in, win, wup, wdn, rope, out):
    with ExitStack() as ctx:
        def sb(name, shape, dt=F32):
            return ctx.enter_context(nc.sbuf_tensor(name, shape, dt))

        def psum(name, shape):
            return ctx.enter_context(nc.psum_tensor(name, shape, F32))

        def sem(name):
            return ctx.enter_context(nc.semaphore(name))

        def dram(name, shape, dt):
            return nc.dram_tensor(name, shape, dt, kind="Internal").ap()

        slots = [psum(f"slot{i}", [P, 3 * HALF]) for i in range(2)]
        attn_out = psum("attn_out", [P, HALF])
        turned_ps = psum("turned_ps", [P, HALF])
        accs = [attn_out, turned_ps]

        xT = sb("xT", [P, KT, TOKENS])
        hidden = xT[:, :, :].rearrange("p k n -> p (k n)").rearrange("p (s n) -> p s n", s=2)
        X = sb("X", [P, TILES, D])
        xn = sb("xn", [P, HT, D])
        xmT = sb("xmT", [P, KT, TOKENS])
        xhT = sb("xhT", [P, KT, TOKENS])
        full = sb("full", [P, KT, HALF])
        parts = sb("parts", [P, PARTS, KT, HALF], BF16)
        qs = sb("qs", [P, HEADS, TOKENS], BF16)
        ks = sb("ks", [P, HEADS, TOKENS], BF16)
        probs = sb("probs", [P, 2, 3 * HALF])
        v = sb("v", [P, TILES * KV_HEADS * 2, VW])
        v1 = v[:, 0:TILES * KV_HEADS, :].rearrange("p (t h) w -> p t h w", t=TILES)
        v2 = v[:, :, :].rearrange("p (t h) w -> p t h w", t=HT)
        o_sb = sb("o_sb", [P, HALF])
        y = sb("y", [P, 2, D])
        yT = sb("yT", [P, 2, KT, SEQ])
        silu = sb("silu", [P, 2, 2 * HALF])
        masks = sb("masks", [P, EXPERTS, TOKENS], BF16)
        neg_max = sb("neg_max", [P, 2, 2 * HEADS])
        max_rest = sb("max_rest", [2 * HEADS, P])
        max_parts = sb("max_parts", [2 * HEADS, 2, PARTS, P], BF16)
        tanh = sb("tanh", [RANK, SEQ])
        modT = sb("modT", [RANK, HALF])
        inv_sum = sb("inv_sum", [P, 2, 8])
        stats = sb("stats", [P, TILES, 6])
        moments = sb("moments", [P, TILES, 2])
        shifted = sb("shifted", [P, TILES])
        rstd = sb("rstd", [P, TILES])
        squares = sb("squares", [P, TILES])
        minus_half = sb("minus_half", [P, TILES])

        wq1_sb, wk1_sb = sb("wq1_sb", [P, KT, D]), sb("wk1_sb", [P, KT, KV_HEADS * HD])
        wv1_sb, wo1_sb = sb("wv1_sb", [P, KT, KV_HEADS * HD]), sb("wo1_sb", [P, KT, D])
        bq1_sb, bk1_sb = sb("bq1_sb", [P, KT]), sb("bk1_sb", [KV_HEADS * HD, 1])
        bv1_sb, bo1_sb = sb("bv1_sb", [P, KV_HEADS * HD]), sb("bo1_sb", [P, D])
        ln1_sb, ln2_sb = sb("ln1_sb", [P, KT]), sb("ln2_sb", [P, KT])
        ctx_sb = sb("ctx_sb", [P, EXPERTS * KT, EF])
        wq2_sb, wk2_sb = sb("wq2_sb", [P, KT, D]), sb("wk2_sb", [P, KT, D])
        wv2_sb, wo2_sb = sb("wv2_sb", [P, KT, D]), sb("wo2_sb", [P, KT, D])
        a_sb, woa_sb = sb("a_sb", [P, KT, RANK]), sb("woa_sb", [P, KT, RANK])
        b_sb = sb("b_sb", [RANK, FF])
        win_sb, wup_sb = sb("win_sb", [P, KT, FF]), sb("wup_sb", [P, KT, FF])
        rope_sb = sb("rope_sb", [P, SEQ])
        ident, ident16 = sb("ident", [P, P]), sb("ident16", [P, P], BF16)
        causal_q = sb("causal_q", [P, GROUP, P], BF16)
        causal_k = sb("causal_k", [P, GROUP, P], BF16)

        q_scratch = [dram(f"q_scratch{a}", (PARTS, D, TOKENS), BF16) for a in range(2)]
        k_scratch = [dram(f"k_scratch{a}", (PARTS, D if a else KV_HEADS * HD, TOKENS), BF16) for a in range(2)]
        m_scratch = [dram(f"m_scratch{a}", (PARTS, BATCHES, 2 * HEADS, P), BF16) for a in range(2)]

        slot_full = [sem(f"slot_full{i}") for i in range(2)]
        slot_free = [sem(f"slot_free{i}") for i in range(2)]
        in_proj1, in_v1, in_x, in_ids, in_attn, in_ctx, in_attn2, in_ffn, in_down = (
            sem(n) for n in ("in_proj1", "in_v1", "in_x", "in_ids", "in_attn", "in_ctx", "in_attn2",
                             "in_ffn", "in_down"))
        consts_ready = sem("consts_ready")
        masks_ready, v_cleared, ones_ready = sem("masks_ready"), sem("v_cleared"), sem("ones_ready")
        bias_added = sem("bias_added")
        part0_ready, rest_ready, part1_ready, split_done, parts_stored = (
            sem(n) for n in ("part0_ready", "rest_ready", "part1_ready", "split_done",
                             "parts_stored"))
        stacked = {s: sem("stacked_" + "_".join(map(str, s[1:]))) for s in PLAN if s[0] == "PROJ"}
        max_stored = sem("max_stored")
        max_stacked = {s: sem("max_stacked_" + "_".join(map(str, s[1:]))) for s in PLAN if s[0] == "MAXT"}
        pv_done, evac_done, turn_done, y_ready = (
            sem(n) for n in ("pv_done", "evac_done", "turn_done", "y_ready"))
        tanh_ready = sem("tanh_ready")
        bank_read_act, bank_read_dve = sem("bank_read_act"), sem("bank_read_dve")
        z_ready, var_ready, rstd_ready, norm_ready, squares_ready = (
            sem(n) for n in ("z_ready", "var_ready", "rstd_ready", "norm_ready", "squares_ready"))
        silu_ready, masked_ready, down_done = (sem(n) for n in ("silu_ready", "masked_ready", "down_done"))
        out_stored = sem("out_stored")
        pool_chain, dve_chain = sem("pool_chain"), sem("dve_chain")

        def slot_of(step):
            return slots[RING_AT[step][0]]

        def filled(eng, step):
            slot, value, _ = RING_AT[step]
            eng.wait_ge(slot_full[slot], value)

        def release(ins, step):
            ins.then_inc(slot_free[RING_AT[step][0]], 1)

        def released(eng, step):
            slot, _, before = RING_AT[step]
            eng.wait_ge(slot_free[slot], before + RING[step[0]])

        def chained(eng, semaphore):
            count = [0]

            def link(ins):
                count[0] += 1
                ins.then_inc(semaphore, 1)
                eng.wait_ge(semaphore, count[0])
            return link

        def norm_tiles(kind, i):
            return range(2 * i, 2 * i + 2) if kind == "ln1" else range(HT * i, HT * i + HT)

        def cols_of(u):
            return slice(HALF * u, HALF * (u + 1))

        block = ctx.enter_context(nc.Block())

        @block.sync
        def _(sp):
            sp.dma_start(wq1_sb[:], wq1).then_inc(in_proj1, DMA_DONE)
            sp.dma_start(xT[:, :, 0:HALF], x_feat[:, :, 0:HALF]).then_inc(in_proj1, DMA_DONE)
            sp.dma_start(bq1_sb[:], bq1).then_inc(in_proj1, DMA_DONE)
            sp.dma_start(rope_sb[:], rope).then_inc(in_proj1, DMA_DONE)
            sp.dma_start(wk1_sb[:], wk1).then_inc(in_proj1, DMA_DONE)
            sp.dma_start(bk1_sb[:], bk1).then_inc(in_proj1, DMA_DONE)
            sp.dma_start(wv1_sb[:], wv1).then_inc(in_v1, DMA_DONE)
            sp.dma_start(bv1_sb[:], bv1.partition_broadcast(P)).then_inc(in_v1, DMA_DONE)
            sp.dma_start(xT[:, :, HALF:TOKENS], x_feat[:, :, HALF:TOKENS]).then_inc(in_v1, DMA_DONE)
            sp.dma_start(probs[:, 0, 0:TOKENS].bitcast(I32), token_ids.partition_broadcast(P)) \
                .then_inc(in_ids, DMA_DONE)

            def stack(step):
                _, a, u, w = step
                n = NTH[step]
                rows = KV_HEADS * HD if (a, w) == (0, "k") else D
                scratch = (q_scratch if w == "q" else k_scratch)[a]
                sp.wait_ge(split_done, n)
                if rows == D:
                    sp.dma_start(scratch[:, :, cols_of(u)].rearrange("t (m p) n -> p (t m) n", p=P),
                                 parts[:].rearrange("p t m n -> p (t m) n")).then_inc(parts_stored, DMA_DONE)
                else:
                    sp.dma_start(scratch[:, :, cols_of(u)].rearrange("t p n -> p t n"),
                                 parts[0:rows, :, 0, :]).then_inc(parts_stored, DMA_DONE)
                sp.wait_ge(parts_stored, DMA_DONE * n)
                if a == 1:
                    filled(sp, ("ST", 0, BATCHES - 1, GROUPS - 1))
                dst = qs if w == "q" else ks
                for i, term in enumerate(TERMS):
                    part = term[0 if w == "q" else 1]
                    sp.dma_start(dst[HD * i:HD * (i + 1), 0:rows // HD, cols_of(u)],
                                 scratch[part, :, cols_of(u)].rearrange("(h d) n -> d h n", d=HD)) \
                        .then_inc(stacked[step], DMA_DONE)

            def stack_maxima(step):
                _, a, b = step
                n = NTH[step]
                released(sp, step)
                sp.dma_start(m_scratch[a][:, b].rearrange("t r n -> r t n"), max_parts[:, n % 2]) \
                    .then_inc(max_stored, DMA_DONE)
                sp.wait_ge(max_stored, DMA_DONE * n)
                for qt in range(2):
                    c = SEQ * b + P * qt
                    sp.dma_start(qs[STACK:STACK + PARTS, :, c:c + P],
                                 m_scratch[a][:, b, HEADS * qt:HEADS * (qt + 1), :]) \
                        .then_inc(max_stacked[step], DMA_DONE)

            for step in PLAN:
                if step[0] == "CAST":
                    stack(("PROJ", *step[1:]))
                if step == ("V", 0, 0):
                    sp.dma_start(X[:], x_tok).then_inc(in_x, DMA_DONE)
                    sp.dma_start(bo1_sb[:], bo1.partition_broadcast(P)).then_inc(in_x, DMA_DONE)
                if step == ("V", 0, 1):
                    sp.dma_start(wo1_sb[:], wo1).then_inc(in_attn, DMA_DONE)
                    sp.dma_start(wo2_sb[:], wo2).then_inc(in_attn, DMA_DONE)
                    sp.dma_start(a_sb[:], a_in).then_inc(in_attn, DMA_DONE)
                    sp.dma_start(ctx_sb[:], ctx_t).then_inc(in_ctx, DMA_DONE)
                    for dst, src in ((ln1_sb, ln1), (ln2_sb, ln2), (wq2_sb, wq2), (wk2_sb, wk2), (wv2_sb, wv2)):
                        sp.dma_start(dst[:], src).then_inc(in_attn2, DMA_DONE)
                    for dst, src in ((win_sb, win), (wup_sb, wup), (b_sb, b_in)):
                        sp.dma_start(dst[:], src).then_inc(in_ffn, DMA_DONE)
                if step[0] == "MAXT":
                    stack_maxima(step)
                if step == ("ST", 1, 0, 0):
                    sp.wait_ge(down_done, NTH["DOWN", "moe", 1, EXPERTS - 1])
                    sp.dma_start(ctx_sb[:], wdn).then_inc(in_down, DMA_DONE)
                if step[0] == "OUT":
                    u = step[1]
                    sp.wait_ge(norm_ready, NTH["NORM", "ln3", u])
                    sp.dma_start(out[:, HT * u:HT * (u + 1), :], X[:, HT * u:HT * (u + 1), :]) \
                        .then_inc(out_stored, DMA_DONE)
            sp.wait_ge(out_stored, DMA_DONE * HALVES)

        @block.gpsimd
        def _(pool):
            link = chained(pool, pool_chain)
            link(pool.memset(ident[:], 0.0))
            link(pool.memset(ident16[:], 0.0))
            link(pool.memset(causal_q[:], 0.0))
            link(pool.memset(causal_k[:], 0.0))
            for m in (ident, ident16):
                link(pool.affine_select(out=m[:], in_=m[:], compare_op=ALU.not_equal, fill=1.0, base=0,
                                        pattern=[[-1, P]], channel_multiplier=1))
            link(pool.affine_select(out=causal_q[:], in_=causal_q[:], compare_op=ALU.is_ge, fill=MASKED, base=0,
                                    pattern=[[0, GROUP], [-1, P]], channel_multiplier=1))
            link(pool.affine_select(out=causal_k[:], in_=causal_k[:], compare_op=ALU.is_ge, fill=MASKED, base=0,
                                    pattern=[[0, GROUP], [1, P]], channel_multiplier=-1))
            pool.memset(minus_half[:], -0.5).then_inc(consts_ready, 1)
            pool.wait_ge(consts_ready, 1)
            link(pool.memset(v[:], 0.0))
            pool.memset(v[:, :, HD:HD + 1], 1.0).then_inc(v_cleared, 1)
            pool.wait_ge(v_cleared, 1)
            pool.memset(ks[STACK:STACK + PARTS, :, :].rearrange("p h n -> p (h n)").bitcast(F32), ONES_PAIR) \
                .then_inc(ones_ready, 1)
            pool.wait_ge(ones_ready, 1)

            def split(step, last):
                _, a, u, w = step
                n = NTH[step]
                rows, mt = (KV_HEADS * HD, 1) if (a, w) == (0, "k") else (P, KT)
                f = full[0:rows, 0:mt, :]
                if not last:
                    pool.wait_ge(part0_ready, n)
                    pool.tensor_tensor(f, f, parts[0:rows, 0, 0:mt, :], ALU.subtract).then_inc(rest_ready, 1)
                else:
                    pool.wait_ge(part1_ready, n)
                    pool.tensor_tensor(parts[0:rows, 2, 0:mt, :], f, parts[0:rows, 1, 0:mt, :],
                                       ALU.subtract).then_inc(split_done, 1)

            for step in PLAN:
                kind = step[0]
                if kind == "PROJ":
                    split(step, False)
                if kind == "CAST":
                    split(("PROJ", *step[1:]), True)
                if step == ("V", 0, 1):
                    pool.wait_ge(in_x, 2 * DMA_DONE)
                    for t in range(TILES):
                        ins = pool.tensor_tensor(X[:, t, :], X[:, t, :], bo1_sb[:], ALU.add)
                    ins.then_inc(bias_added, 1)
                if kind == "RSTD":
                    tiles = norm_tiles(*step[1:])
                    s = slice(tiles[0], tiles[-1] + 1)
                    pool.wait_ge(var_ready, NTH[step])
                    pool.tensor_tensor(rstd[:, s], shifted[:, s], minus_half[:, s], ALU.pow) \
                        .then_inc(rstd_ready, 1)
                if kind == "HID" and step[1] == "moe":
                    _, _, u, e = step
                    n = NTH[step]
                    pool.wait_ge(silu_ready, n)
                    pool.wait_ge(masks_ready, 1)
                    s = silu[:, n % 2, :].rearrange("p (f n) -> p f n", f=2)
                    for f in range(2):
                        ins = pool.tensor_tensor(s[:, f, :], s[:, f, :], masks[:, e, cols_of(u)], ALU.mult)
                    ins.then_inc(masked_ready, 1)

        @block.scalar
        def _(act):
            for step in PLAN:
                kind = step[0]
                if kind in ("PROJ", "CAST"):
                    proj = ("PROJ", *step[1:])
                    n = NTH[proj]
                    _, a, u, w = proj
                    rows, mt = (KV_HEADS * HD, 1) if (a, w) == (0, "k") else (P, KT)
                    if kind == "PROJ":
                        released(act, proj)
                        if n > 1:
                            act.wait_ge(parts_stored, DMA_DONE * (n - 1))
                        act.activation(parts[0:rows, 0, 0:mt, :], full[0:rows, 0:mt, :], ACT.Copy) \
                            .then_inc(part0_ready, 1)
                    else:
                        act.wait_ge(rest_ready, n)
                        act.activation(parts[0:rows, 1, 0:mt, :], full[0:rows, 0:mt, :], ACT.Copy) \
                            .then_inc(part1_ready, 1)
                if kind == "ST":
                    n = NTH[step]
                    filled(act, step)
                    if n == 1:
                        act.wait_ge(masks_ready, 1)
                    if n > 2:
                        act.wait_ge(pv_done, n - 2)
                    release(act.activation(probs[:, n % 2, :], slot_of(step)[:], ACT.Exp, scale=SM_SCALE), step)

                if kind == "EVAC":
                    n = NTH[step]
                    act.wait_ge(pv_done, NTH["PV", step[1], step[2], 2 * step[3] + 1])
                    if n > 1:
                        act.wait_ge(turn_done, n - 1)
                    act.activation(o_sb[:], attn_out[:], ACT.Copy).then_inc(evac_done, 1)
                if kind == "YT":
                    n = NTH[step]
                    filled(act, step)
                    if n > 2:
                        a, b = divmod(n - 3, BATCHES)
                        filled(act, ("MOD" if a else "WO", a, b))
                    release(act.activation(yT[:, n % 2].rearrange("p k n -> p (k n)"), slot_of(step)[:, 0:HALF],
                                           ACT.Copy), step)
                if kind == "TR":
                    _, what, u = step
                    filled(act, step)
                    src = slot_of(step)
                    if what == "x1":
                        ins = act.activation(xmT[:, 0, cols_of(u)], src[:, 0:HALF], ACT.Copy)
                    else:
                        act.wait_ge(in_attn2, 5 * DMA_DONE)
                        for k in (1, 0):
                            if k == 0:
                                act.wait_ge(bank_read_dve, u + 1)
                            ins = act.activation(xmT[:, k, cols_of(u)], src[:, HALF * k:HALF * (k + 1)], ACT.Copy,
                                                 scale=ln1_sb[:, k:k + 1])
                            if k == 1:
                                ins.then_inc(bank_read_act, 1)
                    release(ins, step)
                if kind == "HID":
                    n = NTH[step]
                    width = 2 * HALF if step[1] == "moe" else HALF
                    filled(act, step)
                    if n > 2:
                        released(act, step_at("HID", n - 2))
                    act.activation(silu[:, n % 2, 0:width], slot_of(step)[:, 0:width], ACT.Silu) \
                        .then_inc(silu_ready, 1)
                if kind == "MOD":
                    filled(act, step)
                    if NTH[step] > 1:
                        released(act, step_at("MOD", NTH[step] - 1))
                    act.activation(tanh[:], slot_of(step)[0:RANK, 0:SEQ], ACT.Tanh).then_inc(tanh_ready, 1)
                if kind == "NORM" and step[1] == "ln2":
                    act.wait_ge(norm_ready, NTH[step])
                    for j, t in enumerate(norm_tiles(*step[1:])):
                        ins = act.activation(xn[:, j, :], X[:, t, :], ACT.Square, accum_out=squares[:, t:t + 1])

                    ins.then_inc(squares_ready, 1)

        @block.vector
        def _(dve):
            link = chained(dve, dve_chain)
            dve.wait_ge(in_ids, DMA_DONE)
            ids = probs[:, 0, 0:TOKENS].bitcast(I32)
            at_least = probs[:, 1, :]
            for e in range(EXPERTS):
                lo, hi = float(TOKENS_PER_EXPERT * e), float(TOKENS_PER_EXPERT * (e + 1))
                if e == 0:
                    link(dve.tensor_scalar(masks[:, e, :], ids, hi, None, ALU.is_lt))
                elif e == EXPERTS - 1:
                    dve.tensor_scalar(masks[:, e, :], ids, lo, None, ALU.is_ge).then_inc(masks_ready, 1)
                else:
                    link(dve.tensor_scalar(at_least[:, 0:TOKENS], ids, lo, None, ALU.is_ge))
                    link(dve.scalar_tensor_tensor(out=masks[:, e, :], in0=ids, scalar=hi,
                                                  in1=at_least[:, 0:TOKENS], op0=ALU.is_lt, op1=ALU.mult))

            def moments_of(step, tiles, eps, scale=None):
                for t in tiles:
                    ins = dve.bn_stats(stats[:, t, :], X[:, t, :])
                link(ins)
                for t in tiles:
                    ins = dve.bn_aggr(moments[:, t, :], stats[:, t, :])
                link(ins)
                s = slice(tiles[0], tiles[-1] + 1)
                dve.tensor_scalar(shifted[:, s], moments[:, s, 1], eps, None, ALU.add).then_inc(var_ready, 1)

            for step in PLAN:
                kind = step[0]
                if kind == "PROJ":
                    _, a, u, w = step
                    n = NTH[step]
                    src = slot_of(step)
                    filled(dve, step)
                    if n == 1:
                        dve.wait_ge(in_proj1, 6 * DMA_DONE)
                    if n > 1:
                        dve.wait_ge(split_done, n - 1)
                    if a == 1:
                        ins = dve.tensor_copy(full[:].rearrange("p m n -> p (m n)"), src[:, 0:KT * HALF])
                    else:
                        rows, mt = (P, KT) if w == "q" else (KV_HEADS * HD, 1)
                        for m in range(mt):
                            bias = bq1_sb[:, m:m + 1] if w == "q" else bk1_sb[:, 0:1]
                            for j in range(HALF // SEQ):
                                c = slice(SEQ * j, SEQ * (j + 1))
                                ins = dve.scalar_tensor_tensor(
                                    out=full[0:rows, m, c], in0=src[0:rows, HALF * m + SEQ * j:HALF * m + SEQ * (j + 1)],
                                    scalar=bias, in1=rope_sb[0:rows, :], op0=ALU.add, op1=ALU.mult)
                    release(ins, step)
                if kind == "V":
                    _, a, u = step
                    filled(dve, step)
                    dve.wait_ge(v_cleared, 1)
                    src = slot_of(step)
                    if a == 0:
                        dve.wait_ge(in_v1, 3 * DMA_DONE)
                        for t in range(HT):
                            w = KV_HEADS * HD
                            ins = dve.tensor_tensor(
                                v1[:, HT * u + t, :, 0:HD], src[:, w * t:w * (t + 1)].rearrange("p (h d) -> p h d", d=HD),
                                bv1_sb[:].rearrange("p (h d) -> p h d", d=HD), ALU.add)
                    else:
                        last = ("PV", 1, 1, GROUPS - 1) if u else ("PV", 0, BATCHES - 1, GROUPS - 1)
                        dve.wait_ge(pv_done, NTH[last])
                        for t in range(HT):
                            ins = dve.tensor_copy(v2[:, t, :, 0:HD],
                                                  src[:, D * t:D * (t + 1)].rearrange("p (h d) -> p h d", d=HD))
                    release(ins, step)
                if kind == "S":
                    _, a, b, g = step
                    n = NTH["MAXT", a, b]
                    filled(dve, step)
                    if g == 0 and n > 2:
                        filled(dve, step_at("MAXT", n - 2))
                    src = slot_of(step)
                    h = GROUP * g
                    dve.tensor_reduce(neg_max[:, n % 2, HEADS + h:HEADS + h + GROUP],
                                      src[:, 0:GROUP * SEQ].rearrange("p (h k) -> p h k", h=GROUP), AX, ALU.max,
                                      negate=True)
                    ins = dve.tensor_reduce(neg_max[:, n % 2, h:h + GROUP],
                                            src[:, GROUP * SEQ:3 * HALF].rearrange("p (h k) -> p h k", h=GROUP),
                                            AX, ALU.max, negate=True)
                    release(ins, step)
                if kind == "MAXT":
                    n = NTH[step]
                    filled(dve, step)
                    if n > 2:
                        dve.wait_ge(max_stored, DMA_DONE * (n - 2))
                    src = slot_of(step)[0:2 * HEADS, 0:P]
                    m = max_parts[:, n % 2]
                    link(dve.tensor_copy(m[:, 0, :], src))
                    link(dve.tensor_tensor(max_rest[:], src, m[:, 0, :], ALU.subtract))
                    link(dve.tensor_copy(m[:, 1, :], max_rest[:]))
                    release(dve.tensor_tensor(m[:, 2, :], max_rest[:], m[:, 1, :], ALU.subtract), step)
                if kind == "TURN":
                    _, a, b, pair = step
                    n = NTH[step]
                    dve.wait_ge(turn_done, n)
                    if pair == 0 and (a, b) != (0, 0):
                        filled(dve, ("YT", a, b - 1) if b else ("YT", 0, BATCHES - 1))
                    src = turned_ps[:].rearrange("p (q h w) -> p q h w", q=2, w=VW)
                    link(dve.reciprocal(inv_sum[:], src[:, :, :, HD]))
                    w = 2 * GROUP * HD
                    dve.tensor_tensor(y[:, :, w * pair:w * (pair + 1)].rearrange("p q (h d) -> p q h d", d=HD),
                                      src[:, :, :, 0:HD],
                                      inv_sum[:].unsqueeze(3).broadcast_to([P, 2, 8, HD]), ALU.mult) \
                        .then_inc(y_ready, 1)
                if kind == "WO":
                    _, a, b = step
                    filled(dve, step)
                    dve.wait_ge(bias_added, 1)
                    release(dve.tensor_tensor(X[:, 2 * b:2 * b + 2, :], X[:, 2 * b:2 * b + 2, :],
                                              slot_of(step)[:, 0:2 * D].rearrange("p (t n) -> p t n", t=2),
                                              ALU.add), step)
                    released(dve, step)
                if kind == "RSTD":
                    _, what, i = step
                    tiles = norm_tiles(what, i)
                    if what == "ln1":
                        moments_of(step, tiles, LN_EPS)
                    elif what == "rms":
                        dve.wait_ge(squares_ready, i + 1)
                        s = slice(tiles[0], tiles[-1] + 1)
                        dve.tensor_scalar(shifted[:, s], squares[:, s], 1.0 / D, RMS_EPS, ALU.mult, ALU.add) \
                            .then_inc(var_ready, 1)
                    else:
                        dve.wait_ge(down_done, NTH["DOWN", "moe", i, EXPERTS - 1] if what == "ln2"
                                    else NTH["DOWN", "ffn", i, FT - 1])
                        for j in range(2):
                            xs = X[:, tiles[2 * j]:tiles[2 * j] + 2, :].rearrange("p t n -> p (t n)")
                            ins = dve.scalar_tensor_tensor(out=xs, in0=xs, scalar=1.0 if what == "ln2" else 2.0,
                                                           in1=accs[j][:], op0=ALU.mult, op1=ALU.add)
                        ins.then_inc(z_ready, 1)
                        dve.wait_ge(z_ready, i + 1 + (HALVES if what == "ln3" else 0))
                        moments_of(step, tiles, LN_EPS)
                if kind == "NORM":
                    _, what, i = step
                    dve.wait_ge(rstd_ready, NTH[step])
                    if what == "rms" and i:
                        filled(dve, ("TR", "xn", i - 1))
                    for j, t in enumerate(norm_tiles(what, i)):
                        if what == "rms":
                            ins = dve.tensor_scalar(xn[:, j, :], X[:, t, :], rstd[:, t:t + 1], None, ALU.mult)
                        else:
                            ins = dve.tensor_scalar(X[:, t, :], X[:, t, :], moments[:, t, 0:1], rstd[:, t:t + 1],
                                                    ALU.subtract, ALU.mult)
                    ins.then_inc(norm_ready, 1)
                if kind == "TR":
                    _, what, u = step
                    filled(dve, step)
                    src = slot_of(step)
                    if what == "x1":
                        ins = dve.tensor_copy(xmT[:, 1, cols_of(u)], src[:, HALF:2 * HALF])
                    else:
                        dve.wait_ge(in_attn2, 5 * DMA_DONE)
                        for k in (0, 1):
                            if k == 1:
                                dve.wait_ge(bank_read_act, u + 1)
                            ins = dve.tensor_scalar(xhT[:, k, cols_of(u)], src[:, HALF * k:HALF * (k + 1)],
                                                    ln2_sb[:, k:k + 1], None, ALU.mult)
                            if k == 0:
                                ins.then_inc(bank_read_dve, 1)
                    release(ins, step)
                if kind == "HID":
                    _, what, u, i = step
                    n = NTH[step]
                    if n > 2:
                        dve.wait_ge(down_done, n - 2)
                    if what == "moe":
                        dve.wait_ge(masked_ready, n)
                        ins = dve.tensor_tensor(hidden[:, n % 2, :], silu[:, n % 2, :], slot_of(step)[:, 0:2 * HALF],
                                                ALU.mult)
                    else:
                        dve.wait_ge(silu_ready, n)
                        ins = dve.tensor_tensor(hidden[:, n % 2, 0:HALF], silu[:, n % 2, 0:HALF],
                                                slot_of(step)[:, HALF:2 * HALF], ALU.mult)
                    release(ins, step)
                if kind == "MOD":
                    _, a, b = step
                    dve.wait_ge(tanh_ready, NTH[step])
                    release(dve.scalar_tensor_tensor(out=modT[:, SEQ * (b % 2):SEQ * (b % 2 + 1)], in0=tanh[:],
                                                     scalar=MOD_SCALE, in1=slot_of(step)[0:RANK, HALF:HALF + SEQ],
                                                     op0=ALU.mult, op1=ALU.mult), step)
                if kind == "WOA":
                    filled(dve, step)
                    release(dve.tensor_copy(woa_sb[:].rearrange("p k r -> p (k r)"),
                                            slot_of(step)[:, 0:KT * RANK]), step)

        @block.tensor
        def _(pe):
            mm = pe.matmul

            def take(step):
                slot, _, before = RING_AT[step]
                if before:
                    pe.wait_ge(slot_free[slot], before)
                return slots[slot]

            def give(ins, step):
                ins.then_inc(slot_full[RING_AT[step][0]], 1)

            def project(step):
                _, a, u, w = step
                dst = take(step)
                if a == 0:
                    pe.wait_ge(in_proj1, 6 * DMA_DONE)
                    if u:
                        pe.wait_ge(in_v1, 3 * DMA_DONE)
                    x, weights = xT, wq1_sb if w == "q" else wk1_sb
                else:
                    released(pe, ("TR", "xn", u))
                    pe.wait_ge(in_attn2, 5 * DMA_DONE)
                    x, weights = xmT, wq2_sb if w == "q" else wk2_sb
                small = (a, w) == (0, "k")
                rows = KV_HEADS * HD if small else P
                for m in range(1 if small else KT):
                    for k in range(KT):
                        ins = mm(dst[0:rows, HALF * m:HALF * (m + 1)], weights[:, k, P * m:P * m + rows],
                                 x[:, k, cols_of(u)], start=k == 0, stop=k == KT - 1)
                give(ins, step)

            def values(step):
                _, a, u = step
                dst = take(step)
                x, weights, w = (xmT, wv2_sb, D) if a else (xT, wv1_sb, KV_HEADS * HD)
                if a == 0:
                    pe.wait_ge(in_v1, 3 * DMA_DONE)
                for t in range(HT):
                    for k in range(KT):
                        c = HALF * u + P * t
                        ins = mm(dst[:, w * t:w * (t + 1)], x[:, k, c:c + P], weights[:, k, :],
                                 start=k == 0, stop=k == KT - 1)
                give(ins, step)

            def kv(a, h):
                return h if a else h // (HEADS // KV_HEADS)

            def scores(step):
                _, a, b, g = step
                dst = take(step)
                for w in "qk":
                    pe.wait_ge(stacked["PROJ", a, b // 2, w], DMA_DONE * len(TERMS))
                if g == 0 and b == 0 and a == 0:
                    pe.wait_ge(consts_ready, 1)
                c = SEQ * b
                group = dict(stop=False, skip_group_check=True)
                for j in range(GROUP):
                    h = GROUP * g + j
                    mm(dst[:, SEQ * j:SEQ * (j + 1)], qs[0:STACK, h, c + P:c + SEQ], ks[0:STACK, kv(a, h), c:c + SEQ],
                       start=j % 2 == 0, **group)
                for j in range(GROUP):
                    h = GROUP * g + j
                    at = GROUP * SEQ + P * j
                    mm(dst[:, at:at + P], qs[0:STACK, h, c:c + P], ks[0:STACK, kv(a, h), c:c + P],
                       start=j == 0, **group)
                for j in range(0, GROUP, 2):
                    mm(dst[:, SEQ * j:SEQ * (j + 2)].rearrange("p (h k) -> p h k", h=2)[:, :, P:SEQ], ident16[:],
                       causal_q[:, 0:2, :], start=False, stop=True, skip_group_check=True)
                ins = mm(dst[:, GROUP * SEQ:3 * HALF], ident16[:], causal_q[:].rearrange("p h k -> p (h k)"),
                         start=False, stop=True, skip_group_check=True)
                give(ins, step)

            def turn_maxima(step):
                n = NTH[step]
                dst = take(step)
                released(pe, ("S", step[1], step[2], GROUPS - 1))
                give(pe.transpose(dst[0:2 * HEADS, 0:P], neg_max[:, n % 2, :], ident[:]), step)

            def scores_turned(step):
                _, a, b, g = step
                dst = take(step)
                pe.wait_ge(max_stacked["MAXT", a, b], 2 * DMA_DONE)
                if g == 0 and b == 0 and a == 0:
                    pe.wait_ge(ones_ready, 1)
                c, rows = SEQ * b, STACK + PARTS
                group = dict(stop=False, skip_group_check=True)
                early, late = dst[:, 0:GROUP * SEQ], dst[:, GROUP * SEQ:3 * HALF]
                per = 1 if a else 2
                for j in range(0, GROUP, per):
                    h = GROUP * g + j
                    mm(early[:, SEQ * j:SEQ * (j + per)], ks[0:rows, kv(a, h), c:c + P],
                       qs[0:rows, h:h + per, c:c + SEQ], start=j % 2 == 0, **group)
                per = 1 if a else GROUP
                for j in range(0, GROUP, per):
                    h = GROUP * g + j
                    mm(late[:, P * j:P * (j + per)], ks[0:rows, kv(a, h), c + P:c + SEQ],
                       qs[0:rows, h:h + per, c + P:c + SEQ], start=j == 0, **group)
                for j in range(0, GROUP, 2):
                    mm(early[:, SEQ * j:SEQ * (j + 2)].rearrange("p (h q) -> p h q", h=2)[:, :, 0:P], ident16[:],
                       causal_k[:, 0:2, :], start=False, stop=True, skip_group_check=True)
                ins = mm(late, ident16[:], causal_k[:].rearrange("p h q -> p (h q)"),
                         start=False, stop=True, skip_group_check=True)
                give(ins, step)

            def weigh_values(step):
                _, a, b, g = step
                n = NTH["ST", a, b, g]
                released(pe, ("ST", a, b, g))
                if g == 0:
                    released(pe, ("V", a, b // 2))
                if g % 2 == 0:
                    done = NTH["EVAC", a, b, g // 2] - 1
                    if done:
                        pe.wait_ge(evac_done, done)
                    if (a, b, g) in ((1, 0, 0), (1, 2, 0)):
                        pe.wait_ge(z_ready, 2 if b == 0 else 3)
                e = probs[:, n % 2, :]
                early = e[:, 0:GROUP * SEQ].rearrange("p (h q) -> p h q", h=GROUP)
                late = e[:, GROUP * SEQ:3 * HALF].rearrange("p (h q) -> p h q", h=GROUP)
                at = SEQ * (g % 2)
                for kt in range(2):
                    for j in range(GROUP):
                        vt = (v2[:, 2 * (b % 2) + kt, GROUP * g + j, :] if a else v1[:, 2 * b + kt, g, :])
                        ins = mm(attn_out[VW * j:VW * (j + 1), at + P * kt:at + SEQ], vt,
                                 late[:, j, :] if kt else early[:, j, :],
                                 start=kt == 0 and g % 2 == 0, stop=kt == 1, skip_group_check=True,
                                 tile_position=(0, VW * j))
                ins.then_inc(pv_done, 1)

            def turn_outputs(step):
                n = NTH[step]
                pe.wait_ge(evac_done, n)
                if n > 1:
                    pe.wait_ge(y_ready, n - 1)
                for qt in range(2):
                    for gg in range(2):
                        src = SEQ * gg + P * qt
                        dst = P * (2 * qt + gg)
                        ins = pe.transpose(turned_ps[:, dst:dst + P], o_sb[:, src:src + P], ident[:])
                ins.then_inc(turn_done, 1)

            def turn_y(step):
                _, a, b = step
                dst = take(step)
                pe.wait_ge(y_ready, NTH["TURN", a, b, 1])
                for k in range(KT):
                    for qt in range(2):
                        at = SEQ * k + P * qt
                        ins = pe.transpose(dst[:, at:at + P], y[:, qt, P * k:P * (k + 1)], ident[:])
                give(ins, step)

            def output_product(step):
                _, a, b = step
                dst = take(step)
                n = NTH["YT", a, b]
                released(pe, ("YT", a, b))
                pe.wait_ge(in_attn, 3 * DMA_DONE)
                for qt in range(2):
                    for k in range(KT):
                        ins = mm(dst[:, D * qt:D * (qt + 1)], yT[:, n % 2, k, P * qt:P * (qt + 1)], wo1_sb[:, k, :],
                                 start=k == 0, stop=k == KT - 1)
                give(ins, step)

            def modulation(step):
                _, a, b = step
                dst = take(step)
                n = NTH["YT", a, b]
                for k in range(KT):
                    mm(dst[0:RANK, HALF:HALF + SEQ], a_sb[:, k, :], xhT[:, k, SEQ * b:SEQ * (b + 1)],
                       start=k == 0, stop=k == KT - 1)
                released(pe, ("YT", a, b))
                released(pe, ("WOA",))
                for k in range(KT):
                    ins = mm(dst[0:RANK, 0:SEQ], woa_sb[:, k, :], yT[:, n % 2, k, :], start=k == 0, stop=k == KT - 1)
                give(ins, step)

            def fold(step):
                dst = take(step)
                pe.wait_ge(in_attn, 3 * DMA_DONE)
                for m in range(KT):
                    for k in range(KT):
                        ins = mm(dst[:, RANK * m:RANK * (m + 1)], wo2_sb[:, k, P * m:P * (m + 1)], a_sb[:, k, :],
                                 start=k == 0, stop=k == KT - 1)
                give(ins, step)

            def turn_tokens(step):
                _, what, u = step
                dst = take(step)
                pe.wait_ge(norm_ready, NTH["NORM", "ln1", 2 * u + 1] if what == "x1" else NTH["NORM", "rms", u])
                for k in range(KT):
                    for t in range(HT):
                        src = (X[:, HT * u + t] if what == "x1" else xn[:, t])[:, P * k:P * (k + 1)]
                        at = HALF * k + P * t
                        ins = pe.transpose(dst[:, at:at + P], src, ident[:])
                give(ins, step)

            def hidden_products(step):
                _, what, u, i = step
                dst = take(step)
                if what == "moe":
                    if i == 0:
                        released(pe, ("TR", "x1", u))
                        pe.wait_ge(in_ctx, DMA_DONE)
                    for f in range(2):
                        for k in range(KT):
                            ins = mm(dst[:, HALF * f:HALF * (f + 1)], ctx_sb[:, KT * i + k, P * f:P * (f + 1)],
                                     xmT[:, k, cols_of(u)], start=k == 0, stop=k == KT - 1)
                else:
                    if i == 0:
                        released(pe, ("MOD", 1, 2 * u + 1))
                        pe.wait_ge(in_ffn, 3 * DMA_DONE)
                    f = slice(P * i, P * (i + 1))
                    for k in range(KT):
                        mm(dst[:, 0:HALF], win_sb[:, k, f], xhT[:, k, cols_of(u)], start=k == 0, stop=False)
                    mm(dst[:, 0:HALF], b_sb[:, f], modT[:], start=False, stop=True)
                    for k in range(KT):
                        ins = mm(dst[:, HALF:2 * HALF], wup_sb[:, k, f], xhT[:, k, cols_of(u)],
                                 start=k == 0, stop=k == KT - 1)
                give(ins, step)

            def down_product(step):
                _, what, u, i = step
                n = NTH["HID", what, u, i]
                released(pe, ("HID", what, u, i))
                if i == 0:
                    if what == "moe":
                        if u == 0:
                            pe.wait_ge(evac_done, NTH["EVAC", 0, BATCHES - 1, 1])
                            pe.wait_ge(y_ready, NTH["TURN", 0, BATCHES - 1, 1])
                        else:
                            pe.wait_ge(z_ready, 1)
                    else:
                        pe.wait_ge(evac_done, NTH["EVAC", 1, 2 * u + 1, 1])
                        pe.wait_ge(y_ready, NTH["TURN", 1, 2 * u + 1, 1])
                        pe.wait_ge(in_down, DMA_DONE)
                ktiles, last = (2, EXPERTS - 1) if what == "moe" else (1, FT - 1)
                for k in range(ktiles):
                    for t in range(HT):
                        at = HALF * k + P * t
                        ins = mm(accs[t // 2][:, D * (t % 2):D * (t % 2 + 1)], hidden[:, n % 2, at:at + P],
                                 ctx_sb[:, ktiles * i + k, :], start=i == 0 and k == 0 and t % 2 == 0,
                                 stop=i == last and k == ktiles - 1, skip_group_check=True)
                ins.then_inc(down_done, 1)

            parts_of = {"PROJ": project, "V": values, "S": scores, "MAXT": turn_maxima, "ST": scores_turned,
                        "PV": weigh_values, "TURN": turn_outputs, "YT": turn_y, "WO": output_product,
                        "MOD": modulation, "WOA": fold, "TR": turn_tokens, "HID": hidden_products,
                        "DOWN": down_product}
            for step in PLAN:
                if step[0] in parts_of:
                    parts_of[step[0]](step)


def rope_table():
    inv = np.float32(10000.0) ** (np.float32(-2.0) * np.arange(HD // 2, dtype=np.float32) / np.float32(HD))
    theta = np.arange(SEQ, dtype=np.float32)[:, None] * inv[None, :].astype(np.float32)
    table = np.cos(theta) + np.sin(theta)
    return np.ascontiguousarray(np.tile(table.T, (P // (HD // 2), 1)).astype(np.float32))


def kernel(**inputs):
    import concourse.bacc as bacc
    from concourse.bass_utils import run_bass_kernel_spmd

    g = {n: np.asarray(a) for n, a in inputs.items()}

    def weight(name):
        w = g[name]
        return w.T.reshape(-1, P, w.shape[0]).transpose(1, 0, 2)

    def columns(name):
        return g[name].reshape(-1, P).T

    x = g["x"].reshape(TOKENS, D)
    arrays = {
        "x_tok": x.reshape(TILES, P, D).transpose(1, 0, 2),
        "x_feat": x.T.reshape(KT, P, TOKENS).transpose(1, 0, 2),
        "token_ids": g["itok_BxS_13_99985"].reshape(TOKENS),
        "ctx_t": g["ctx_2048"].transpose(0, 2, 1).reshape(EXPERTS * KT, P, EF).transpose(1, 0, 2),
        "wq1": weight("L0_attn_Wq"), "bq1": columns("L0_attn_bq"),
        "wk1": weight("L0_attn_Wk"), "bk1": g["L0_attn_bk"].reshape(-1, 1),
        "wv1": weight("L0_attn_Wv"), "bv1": g["L0_attn_bv"],
        "wo1": weight("L0_attn_Wo"), "bo1": g["L0_attn_bo"],
        "ln1": columns("L0_ffn_ln1_w"), "ln2": columns("L0_ffn_ln2_w"),
        "wq2": weight("L0_ffn_Wq"), "wk2": weight("L0_ffn_Wk"), "wv2": weight("L0_ffn_Wv"),
        "wo2": g["L0_ffn_Wo"].reshape(KT, P, D).transpose(1, 0, 2),
        "a_in": g["L0_ffn_A"].reshape(KT, P, RANK).transpose(1, 0, 2), "b_in": g["L0_ffn_B"],
        "win": weight("L0_ffn_W_in_base"), "wup": weight("L0_ffn_W_up_base"), "wdn": weight("L0_ffn_W_down"),
        "rope": rope_table(),
    }
    nc = bacc.Bacc("TRN2", target_bir_lowering=False, num_devices=1)
    args = []
    for name, a in arrays.items():
        a = arrays[name] = np.ascontiguousarray(a)
        args.append(nc.dram_tensor(name, a.shape, mybir.dt.from_np(a.dtype), kind="ExternalInput").ap())
    args.append(nc.dram_tensor("out", (P, TILES, D), F32, kind="ExternalOutput").ap())
    decoder_layer(nc, *args)
    got = run_bass_kernel_spmd(nc, [arrays], core_ids=[0]).results[0]["out"]
    return np.ascontiguousarray(got.transpose(1, 0, 2)).reshape(BATCHES, SEQ, D)
```

```python
from contextlib import ExitStack

import numpy as np

import concourse.bass as bass
from concourse import mybir

P = 128
BATCHES, SEQ, D = 4, 256, 256
TOKENS = BATCHES * SEQ
TILES = TOKENS // P
HALF = 512
HALVES = TOKENS // HALF
HT = HALF // P
KT = D // P
HEADS, HD = 16, 16
KV_HEADS = 4
GROUP = 4
GROUPS = HEADS // GROUP
VW = 32
EXPERTS, EF = 4, 256
TOKENS_PER_EXPERT = 12500 // EXPERTS
FF = 1024
FT = FF // P
RANK = 16
MOD_SCALE = 0.1
LN_EPS, RMS_EPS = 1e-5, 1e-6
SM_SCALE = HD ** -0.5
MASKED = -1e30
PARTS = 3
RUNS = [3, 2, 1]
STACK = HD * sum(RUNS)
AHEAD = 6
BUFFERS = 3
EARLY = 2
DMA_DONE = 16
COPIES = 3
WIDE = 3 * D

F32, F32R, BF16, I32 = mybir.dt.float32, mybir.dt.float32r, mybir.dt.bfloat16, mybir.dt.int32
ALU = mybir.AluOpType
ACT = mybir.ActivationFunctionType
AX = mybir.AxisListType.X
ONES_PAIR = float(np.array([0x3F803F80], np.uint32).view(np.float32)[0])

RING = {"PROJ": 1, "V": 1, "S": 1, "MAXT": 1, "ST": 1, "YT": 1, "WO": 1, "TR": 2, "HID": 1, "MOD": 1,
        "WOA": 1}


def make_plan():
    plan, later = [], []

    def add(*step):
        plan.append(step)

    def one_later():
        if later:
            add(*later.pop(0))

    def flush():
        while later:
            one_later()

    def units(a, u):
        if a == 0:
            return [("PROJ", 0, u, "k", 0), ("PROJ", 0, u, "q", 0), ("PROJ", 0, u, "q", 1)]
        return [("PROJ", 1, u, w, m) for m in range(KT) for w in "kq"]

    def norm_steps(*kinds_at):
        return [(kind, *at) for at in kinds_at for kind in ("RSTD", "NORM")]

    def attend(a, fill):
        order = [(b, g) for b in range(BATCHES) for g in range(GROUPS)]
        ahead = order[AHEAD:]
        projected = max([t for t in fill if ("PROJ", a, 1, "q", 1) in fill[t]], default=-1) + 1
        maxima, turns = [], []
        for t in range(len(order) + 1):
            if maxima:
                add("MAXT", a, maxima.pop())
            for _ in range(2):
                at = len(order) - len(ahead)
                if ahead and at <= t + AHEAD and (at < len(order) // 2 or t > projected):
                    b, g = ahead.pop(0)
                    add("S", a, b, g)
                    if g == GROUPS - 1:
                        maxima.append(b)
            if t < len(order):
                add("ST", a, *order[t])
            if turns:
                add(*turns[0])
                if turns.pop()[3]:
                    later.extend(after(a, order[t - 2][0]))
            if t:
                b, g = order[t - 1]
                add("PV", a, b, g)
                if g % 2:
                    add("EVAC", a, b, g // 2)
                    turns.append(("TURN", a, b, g // 2))
            one_later()
            for step in fill.get(t, ()):
                add(*step)
        later.extend(turns + after(a, BATCHES - 1))

    def after(a, b):
        if a == 0:
            return [("YT", a, b), ("WO", a, b), *norm_steps(("ln1", b))]
        return [("YT", a, b), ("MOD", a, b)]

    for step in units(0, 0):
        add(*step)
    add("V", 0, 0)
    second = units(0, 1)
    add(*second[0])
    add("V", 0, 1)
    for g in range(GROUPS):
        add("S", 0, 0, g)
    add(*second[1])
    add("MAXT", 0, 0)
    add("S", 0, 1, 0)
    add("S", 0, 1, 1)
    add(*second[2])
    add("WOA")
    attend(0, {**{4 + 2 * e: [("SPLIT", "ctx", e)] for e in range(EXPERTS)}, 12: [("TR", "x1", 0)]})

    add("HID", "moe", 0, 0)
    one_later()
    add("HID", "moe", 0, 1)
    add("MULT", "moe", 0, 0)
    one_later()
    add("MULT", "moe", 0, 1)
    add("DOWN", "moe", 0, 0)
    one_later()
    one_later()
    add("HID", "moe", 0, 2)
    one_later()
    add("MULT", "moe", 0, 2)
    add("DOWN", "moe", 0, 1)
    add("TR", "x1", 1)
    add("HID", "moe", 0, 3)
    add("MULT", "moe", 0, 3)
    add("DOWN", "moe", 0, 2)
    add("HID", "moe", 1, 0)
    add("DOWN", "moe", 0, 3)
    add("MULT", "moe", 1, 0)
    add("RSTD", "ln2", 0)
    add("NORM", "ln2", 0)
    add("HID", "moe", 1, 1)
    add("MULT", "moe", 1, 1)
    add("DOWN", "moe", 1, 0)
    add("HID", "moe", 1, 2)
    add("TR", "xn", 0)
    add("MULT", "moe", 1, 2)
    add("DOWN", "moe", 1, 1)
    first = units(1, 0)
    add(*first[0])
    add(*first[1])
    add("HID", "moe", 1, 3)
    add("RESIDUAL", 0)
    add("DOWN", "moe", 1, 2)
    add("MULT", "moe", 1, 3)
    add(*first[2])
    add(*first[3])
    add("V", 1, 0)
    add("DOWN", "moe", 1, 3)
    add("RSTD", "ln2", 1)
    add("S", 1, 0, 0)
    add("S", 1, 0, 1)
    add("NORM", "ln2", 1)
    add("S", 1, 0, 2)
    add("S", 1, 0, 3)
    add("TR", "xn", 1)
    add("RESIDUAL", 1)
    add("MAXT", 1, 0)
    add("S", 1, 1, 0)
    add("S", 1, 1, 1)
    second = units(1, 1)
    add(*second[0])
    add(*second[1])
    attend(1, {0: [second[2]], 1: [second[3]], 2 * GROUPS: [("V", 1, 1)],
               11: [("SPLIT", "x", 0)], 12: [("SPLIT_B",)],
               13: [("SPLIT", "w", 0)], 14: [("SPLIT", "w", 1)]})

    tiles = [(u, f) for u in range(HALVES) for f in range(FT)]
    for i, (u, f) in enumerate(tiles):
        add("HID", "ffn", u, f)
        add("MULT", "ffn", u, f)
        if u == 0 and f + EARLY < FT:
            add("SPLIT", "w", f + EARLY)
        one_later()
        if i:
            add("DOWN", "ffn", *tiles[i - 1])
        if (u, f) == (0, FT // 2):
            add("SPLIT", "x", 1)
        if (u, f) == (1, 0):
            add("RSTD", "ln3", 0)
            add("RSTD", "ln3", 1)
            later.extend((kind, "ln3", pair) for pair in range(2) for kind in ("NORM", "OUT"))
    add("DOWN", "ffn", *tiles[-1])
    flush()
    for pair in (2, 3):
        add("RSTD", "ln3", pair)
    for pair in (2, 3):
        add("NORM", "ln3", pair)
        add("OUT", "ln3", pair)
    flush()
    return plan


PLAN = make_plan()


def count_steps():
    nth, ring, seen, filled, released = {}, {}, {}, [0, 0], [0, 0]
    for step in PLAN:
        kind = step[0]
        seen[kind] = seen.get(kind, 0) + 1
        nth[step] = seen[kind]
        if kind in RING:
            slot = sum(filled) % 2
            filled[slot] += 1
            ring[step] = (slot, filled[slot], released[slot])
            released[slot] += RING[kind]
    return nth, ring


NTH, RING_AT = count_steps()


def step_at(kind, n):
    return [s for s in PLAN if s[0] == kind][n - 1]


def rows_of(step):
    return KV_HEADS * HD if step[1] == 0 and step[3] == "k" else P


def step_count(kind, a):
    return sum(s[:2] == (kind, a) for s in PLAN)


def decoder_layer(nc, x_tok, x_feat, token_ids, ctx_t, wq1, bq1, wk1, bk1, wv1, bv1, wo1, bo1, ln1, ln2,
                  wq2, wk2, wv2, wo2, a_in, b_in, w_ffn, rope_in, out):
    with ExitStack() as ctx:
        def sb(name, shape, dt=F32):
            return ctx.enter_context(nc.sbuf_tensor(name, shape, dt))

        def psum(name, shape):
            return ctx.enter_context(nc.psum_tensor(name, shape, F32))

        starts = {}

        def sb_region(name, shape, dt=F32):
            t = sb(name, shape, dt)
            starts[name] = nc.sbuf_base - int(np.prod(shape[1:])) * mybir.dt.size(dt)
            return t

        def over(region, at, name, shape, dt=F32R):
            return nc.alloc_sbuf_tensor_at(name, shape, dt, offset=starts[region] + at)

        def sem(name):
            return ctx.enter_context(nc.semaphore(name))

        def dram(name, shape, dt):
            return nc.dram_tensor(name, shape, dt, kind="Internal").ap()

        slots = [psum(f"slot{i}", [P, 3 * HALF]) for i in range(2)]
        attn_out = psum("attn_out", [P, HALF])
        turned_ps = psum("turned_ps", [P, HALF])
        accs = [attn_out, turned_ps]

        xT = sb_region("xT", [P, KT, TOKENS])
        X = sb("X", [P, TILES, D])
        xn = sb("xn", [P, HT, D])
        ids = xn[:].rearrange("p t n -> p (t n)").bitcast(I32)
        xmT = sb_region("xmT", [P, KT, TOKENS])
        xhT = sb_region("xhT", [P, KT, TOKENS])
        full = sb("full", [P, 2, HALF])
        parts = sb("parts", [P, 2, PARTS, HALF], BF16)
        qs = sb_region("qs", [P, HALVES, HEADS, HALF], BF16)
        ks = sb_region("ks", [P, HALVES, HEADS, HALF], BF16)
        probs = sb_region("probs", [P, BUFFERS, 3 * HALF])
        silu = probs[:].rearrange("p b n -> p (b n)")[:, 0:4 * HALF].rearrange("p (s n) -> p s n", s=2)
        v = sb("v", [P, TILES * KV_HEADS * 2, VW])
        v1 = v[:, 0:TILES * KV_HEADS, :].rearrange("p (t h) w -> p t h w", t=TILES)
        v2 = v[:, :, :].rearrange("p (t h) w -> p t h w", t=HT)
        o_sb = sb_region("o_sb", [P, HALF])
        y = sb("y", [P, 2, D])
        yT = sb_region("yT", [P, 2, KT, SEQ])
        masks = sb_region("masks", [P, EXPERTS, TOKENS], BF16)
        neg_max = sb("neg_max", [P, 2, 2 * HEADS])
        max_rest = sb("max_rest", [2 * HEADS, P])
        max_parts = sb("max_parts", [2 * HEADS, 2, PARTS, P], BF16)
        tanh = sb("tanh", [COPIES * RANK, SEQ])
        modT = sb("modT", [COPIES * RANK, TOKENS], F32R)
        inv_sum = sb("inv_sum", [P, 2, 8])
        stats = sb("stats", [P, TILES, 6])
        moments = sb("moments", [P, TILES, 2])
        shifted = sb("shifted", [P, TILES])
        rstd = sb("rstd", [P, TILES])
        rms = sb("rms", [P, TILES])
        minus_half = sb("minus_half", [P, TILES])

        wq1_sb, wk1_sb = sb("wq1_sb", [P, KT, D]), sb("wk1_sb", [P, KT, KV_HEADS * HD])
        wv1_sb, wo1_sb = sb("wv1_sb", [P, KT, KV_HEADS * HD]), sb("wo1_sb", [P, KT, D])
        bq1_sb, bk1_sb = sb("bq1_sb", [P, KT]), sb("bk1_sb", [KV_HEADS * HD, 1])
        bv1_sb, bo1_sb = sb("bv1_sb", [P, KV_HEADS * HD]), sb("bo1_sb", [P, D])
        ln1_sb, ln2_sb = sb("ln1_sb", [P, KT]), sb("ln2_sb", [P, KT])
        ctx_sb = sb_region("ctx_sb", [P, EXPERTS * KT, EF])
        ctx_h = sb("ctx_h", [P, EXPERTS * KT, EF], F32R)
        ctx_l = sb("ctx_l", [P, EXPERTS * KT, EF], F32R)
        wq2_sb, wk2_sb = sb("wq2_sb", [P, KT, D]), sb("wk2_sb", [P, KT, D])
        wv2_sb, wo2_sb = sb("wv2_sb", [P, KT, D]), sb("wo2_sb", [P, KT, D])
        a_sb, woa_sb = sb("a_sb", [P, KT, COPIES * RANK]), sb("woa_sb", [P, KT, COPIES * RANK])
        b3 = sb("b3", [COPIES * RANK, FF], F32R)
        rope = sb("rope", [P, 2, SEQ])
        ident, ident16 = sb("ident", [P, P]), sb("ident16", [P, P], BF16)
        causal_q = sb("causal_q", [P, GROUP, P], BF16)
        causal_k = sb("causal_k", [P, GROUP, P], BF16)

        kb = 1024
        x1_h = [over("xhT", 0, "x1_h0", [P, KT, HALF]), over("o_sb", 0, "x1_h1", [P, KT, HALF])]
        x1_l = [over("xhT", 4 * kb, "x1_l0", [P, KT, HALF]), over("yT", 0, "x1_l1", [P, KT, HALF])]
        hidden_h = [over("xT", 0, "hidden_h0", [P, 2 * HALF]), over("probs", 8 * kb, "hidden_h1", [P, 2 * HALF])]
        hidden_l = [over("xT", 4 * kb, "hidden_l0", [P, 2 * HALF]), over("probs", 12 * kb, "hidden_l1", [P, 2 * HALF])]
        w_raw = over("ctx_sb", 0, "w_raw", [P, FT, WIDE], F32)
        b_raw = over("masks", 0, "b_raw", [COPIES * RANK, FF], F32)
        w_l = over("ctx_sb", 0, "w_l", [P, FT, WIDE])
        w_early, w_late = over("xmT", 0, "w_early", [P, EARLY, WIDE]), over("ks", 0, "w_late", [P, FT - EARLY, WIDE])
        w_h = [w_early[:, f, :] if f < EARLY else w_late[:, f - EARLY, :] for f in range(FT)]
        xh_h, xh_l = over("xT", 0, "xh_h", [P, KT, TOKENS]), over("xhT", 0, "xh_l", [P, KT, TOKENS])
        ffn_hidden_h = [over("qs", 4 * kb * i, f"ffn_hidden_h{i}", [P, HALF]) for i in range(2)]
        ffn_hidden_l = [over("qs", 4 * kb * i + 2 * kb, f"ffn_hidden_l{i}", [P, HALF]) for i in range(2)]

        scratch = {s: dram("scratch_" + "_".join(map(str, s[1:])), (PARTS, rows_of(s), HALF), BF16)
                   for s in PLAN if s[0] == "PROJ"}
        m_scratch = [dram(f"m_scratch{a}", (PARTS, BATCHES, 2 * HEADS, P), BF16) for a in range(2)]

        slot_full = [sem(f"slot_full{i}") for i in range(2)]
        slot_free = [sem(f"slot_free{i}") for i in range(2)]
        in_k1, in_q1, in_rope, in_v1, in_x2, in_x, in_ids, in_attn, in_ctx, in_attn2, in_b = (
            sem(n) for n in ("in_k1", "in_q1", "in_rope", "in_v1", "in_x2", "in_x", "in_ids", "in_attn", "in_ctx", "in_attn2",
                             "in_b"))
        in_w = [sem(f"in_w{f}") for f in range(FT)]
        consts_ready = sem("consts_ready")
        masks_ready, v_cleared, ones_ready = sem("masks_ready"), sem("v_cleared"), sem("ones_ready")
        bias_added = sem("bias_added")
        one_ready, split_done = sem("one_ready"), sem("split_done")
        parts_stored = {s: sem("parts_stored_" + "_".join(map(str, s[1:]))) for s in PLAN if s[0] == "PROJ"}
        stacked = {s: sem("stacked_" + "_".join(map(str, s[1:]))) for s in PLAN if s[0] == "PROJ"}
        max_stored = sem("max_stored")
        max_stacked = {s: sem("max_stacked_" + "_".join(map(str, s[1:]))) for s in PLAN if s[0] == "MAXT"}
        pv_done, evac_done, turn_done, y_ready = (
            sem(n) for n in ("pv_done", "evac_done", "turn_done", "y_ready"))
        tanh_ready = sem("tanh_ready")
        bank_read_act, bank_read_dve = sem("bank_read_act"), sem("bank_read_dve")
        z_ready, var_ready, rstd_ready, norm_ready, xn_ready, x2_ready = (
            sem(n) for n in ("z_ready", "var_ready", "rstd_ready", "norm_ready", "xn_ready", "x2_ready"))
        high_done, low_done, x1_high, hidden_ready, mod_ready = (
            sem(n) for n in ("high_done", "low_done", "x1_high", "hidden_ready", "mod_ready"))
        b_ready, pair_done = sem("b_ready"), sem("pair_done")
        silu_ready, masked_ready, down_done = (sem(n) for n in ("silu_ready", "masked_ready", "down_done"))
        out_stored = sem("out_stored")
        pool_chain, dve_chain = sem("pool_chain"), sem("dve_chain")

        def slot_of(step):
            return slots[RING_AT[step][0]]

        def filled(eng, step):
            slot, value, _ = RING_AT[step]
            eng.wait_ge(slot_full[slot], value)

        def release(ins, step):
            ins.then_inc(slot_free[RING_AT[step][0]], 1)

        def released(eng, step, by=None):
            slot, _, before = RING_AT[step]
            eng.wait_ge(slot_free[slot], before + (by or RING[step[0]]))

        def chained(eng, semaphore):
            count = [0]

            def link(ins):
                count[0] += 1
                ins.then_inc(semaphore, 1)
                eng.wait_ge(semaphore, count[0])
            return link

        def split_parts(step):
            _, what, i = step
            if what == "ctx":
                return tuple(t[:, KT * i:KT * (i + 1), :] for t in (ctx_sb, ctx_h, ctx_l))
            if what == "w":
                return w_raw[:, i, :], w_h[i], w_l[:, i, :]
            return tuple(t[:, :, cols_of(i)] for t in (xhT, xh_h, xh_l))

        def hidden_parts(what, n):
            pair = (hidden_h, hidden_l) if what == "moe" else (ffn_hidden_h, ffn_hidden_l)
            return pair[0][n % 2], pair[1][n % 2]

        def norm_tiles(kind, i):
            return range(HT * i, HT * i + HT) if kind == "ln2" else range(2 * i, 2 * i + 2)

        def cols_of(u):
            return slice(HALF * u, HALF * (u + 1))

        block = ctx.enter_context(nc.Block())

        @block.sync
        def _(sp):
            sp.dma_start(wk1_sb[:], wk1).then_inc(in_k1, DMA_DONE)
            sp.dma_start(xT[:, :, 0:HALF], x_feat[:, :, 0:HALF]).then_inc(in_k1, DMA_DONE)
            sp.dma_start(wq1_sb[:], wq1).then_inc(in_q1, DMA_DONE)

            def store_parts(step):
                n = NTH[step]
                sp.wait_ge(split_done, n)
                sp.dma_start(scratch[step].rearrange("t p n -> p t n"), parts[0:rows_of(step), n % 2]) \
                    .then_inc(parts_stored[step], DMA_DONE)

            def stack(step):
                _, a, u, w, m = step
                sp.wait_ge(parts_stored[step], DMA_DONE)
                if a == 1:
                    filled(sp, ("ST", 0, BATCHES - 1, GROUPS - 1))
                heads = rows_of(step) // HD
                dst = (qs if w == "q" else ks)[:, u, P // HD * m:P // HD * m + heads, :].rearrange("p h n -> p (h n)")
                src = scratch[step].rearrange("t (d h) n -> (t d) (h n)", h=heads)
                row = 0
                for run in RUNS:
                    first = 0 if w == "q" else PARTS - run
                    sp.dma_start(dst[row:row + HD * run], src[HD * first:HD * (first + run)]) \
                        .then_inc(stacked[step], DMA_DONE)
                    row += HD * run

            def stack_maxima(step):
                _, a, b = step
                n = NTH[step]
                released(sp, step)
                sp.dma_start(m_scratch[a][:, b].rearrange("t r n -> r t n"), max_parts[:, n % 2]) \
                    .then_inc(max_stored, DMA_DONE)
                sp.wait_ge(max_stored, DMA_DONE * n)
                for qt in range(2):
                    c = SEQ * (b % 2) + P * qt
                    sp.dma_start(qs[STACK:STACK + PARTS, b // 2, :, c:c + P],
                                 m_scratch[a][:, b, HEADS * qt:HEADS * (qt + 1), :]) \
                        .then_inc(max_stacked[step], DMA_DONE)

            for step in PLAN:
                if step[0] == "PROJ":
                    store_parts(step)
                    if step[3] == "q":
                        if step[:3] + ("k", step[4]) in NTH:
                            stack(step[:3] + ("k", step[4]))
                        stack(step)
                if step == ("ST", 0, 1, 0):
                    sp.dma_start(ctx_sb[:], ctx_t).then_inc(in_ctx, DMA_DONE)
                    for dst, src in ((ln1_sb, ln1), (ln2_sb, ln2), (wq2_sb, wq2), (wk2_sb, wk2), (wv2_sb, wv2)):
                        sp.dma_start(dst[:], src).then_inc(in_attn2, DMA_DONE)
                if step[0] == "MAXT":
                    stack_maxima(step)
                if step[0] == "ST" and step[1] == 1 and 6 <= GROUPS * step[2] + step[3] < 6 + FT:
                    f = GROUPS * step[2] + step[3] - 6
                    if f == 0:
                        sp.wait_ge(down_done, NTH["DOWN", "moe", 1, EXPERTS - 1])
                        for i in range(COPIES):
                            sp.dma_start(b_raw[RANK * i:RANK * (i + 1), :], b_in).then_inc(in_b, DMA_DONE)
                    sp.dma_start(w_raw[:, f, :], w_ffn[:, f, :]).then_inc(in_w[f], DMA_DONE)
                if step[0] == "OUT":
                    pair = step[2]
                    sp.wait_ge(norm_ready, NTH["NORM", "ln3", pair] - HALVES)
                    sp.dma_start(out[:, 2 * pair:2 * pair + 2, :], X[:, 2 * pair:2 * pair + 2, :]) \
                        .then_inc(out_stored, DMA_DONE)
            sp.wait_ge(out_stored, DMA_DONE * TILES // 2)

        @block.gpsimd
        def _(pool):
            link = chained(pool, pool_chain)
            link(pool.memset(ident[:], 0.0))
            link(pool.memset(ident16[:], 0.0))
            link(pool.memset(causal_q[:], 0.0))
            link(pool.memset(causal_k[:], 0.0))
            for m in (ident, ident16):
                link(pool.affine_select(out=m[:], in_=m[:], compare_op=ALU.not_equal, fill=1.0, base=0,
                                        pattern=[[-1, P]], channel_multiplier=1))
            link(pool.affine_select(out=causal_q[:], in_=causal_q[:], compare_op=ALU.is_ge, fill=MASKED, base=0,
                                    pattern=[[0, GROUP], [-1, P]], channel_multiplier=1))
            link(pool.affine_select(out=causal_k[:], in_=causal_k[:], compare_op=ALU.is_ge, fill=MASKED, base=0,
                                    pattern=[[0, GROUP], [1, P]], channel_multiplier=-1))
            pool.memset(minus_half[:], -0.5).then_inc(consts_ready, 1)
            pool.wait_ge(consts_ready, 1)
            link(pool.memset(v[:], 0.0))
            pool.memset(v[:, :, HD:HD + 1], 1.0).then_inc(v_cleared, 1)
            pool.wait_ge(v_cleared, 1)
            pool.memset(ks[STACK:STACK + PARTS].rearrange("p u h n -> p (u h n)").bitcast(F32), ONES_PAIR) \
                .then_inc(ones_ready, 1)
            pool.wait_ge(ones_ready, 1)

            def expert_masks():
                pool.wait_ge(in_ids, DMA_DONE)
                at_least = masks[:, EXPERTS - 1, :]
                for e in range(EXPERTS - 1):
                    lo, hi = float(TOKENS_PER_EXPERT * e), float(TOKENS_PER_EXPERT * (e + 1))
                    link(pool.tensor_scalar(masks[:, e, :], ids[:], hi, None, ALU.is_lt))
                    if e:
                        link(pool.tensor_scalar(at_least, ids[:], lo, None, ALU.is_ge))
                        link(pool.tensor_tensor(masks[:, e, :], masks[:, e, :], at_least, ALU.mult))
                pool.tensor_scalar(at_least, ids[:], float(TOKENS_PER_EXPERT * (EXPERTS - 1)), None, ALU.is_ge) \
                    .then_inc(masks_ready, 1)

            for step in PLAN:
                kind = step[0]
                if step == ("V", 0, 1):
                    expert_masks()
                    pool.wait_ge(in_x, 2 * DMA_DONE)
                    for t in range(TILES):
                        ins = pool.tensor_tensor(X[:, t, :], X[:, t, :], bo1_sb[:], ALU.add)
                    ins.then_inc(bias_added, 1)
                if kind == "RSTD":
                    tiles = norm_tiles(*step[1:])
                    s = slice(tiles[0], tiles[-1] + 1)
                    pool.wait_ge(var_ready, NTH[step])
                    ins = pool.tensor_tensor(rstd[:, s], shifted[:, s], minus_half[:, s], ALU.pow)
                    if step[1] == "ln2":
                        link(ins)
                        r = rms[:, s]
                        link(pool.tensor_tensor(r, rstd[:, s], rstd[:, s], ALU.mult))
                        link(pool.tensor_tensor(r, r, moments[:, s, 1], ALU.mult))
                        link(pool.tensor_scalar(r, r, RMS_EPS, None, ALU.add))
                        link(pool.tensor_tensor(r, r, minus_half[:, s], ALU.pow))
                        ins = pool.tensor_tensor(r, r, rstd[:, s], ALU.mult)
                    ins.then_inc(rstd_ready, 1)
                if kind == "RESIDUAL":
                    pool.wait_ge(xn_ready, step[1] + 1)
                    for t in norm_tiles("ln2", step[1]):
                        ins = pool.tensor_scalar(X[:, t, :], X[:, t, :], moments[:, t, 0:1], rstd[:, t:t + 1],
                                                 ALU.subtract, ALU.mult)
                    ins.then_inc(x2_ready, 1)
                if kind == "HID" and step[1] == "moe":
                    _, _, u, e = step
                    n = NTH[step]
                    pool.wait_ge(silu_ready, n)
                    pool.wait_ge(masks_ready, 1)
                    s = silu[:, n % 2, :].rearrange("p (f n) -> p f n", f=2)
                    for f in range(2):
                        pool.tensor_tensor(s[:, f, :], s[:, f, :], masks[:, e, cols_of(u)], ALU.mult) \
                            .then_inc(masked_ready, 1)

        @block.scalar
        def _(act):
            act.dma_start(rope[:], rope_in).then_inc(in_rope, DMA_DONE)
            act.dma_start(bk1_sb[:], bk1).then_inc(in_rope, DMA_DONE)
            act.dma_start(bq1_sb[:], bq1).then_inc(in_rope, DMA_DONE)
            act.dma_start(wv1_sb[:], wv1).then_inc(in_v1, DMA_DONE)
            act.dma_start(bv1_sb[:], bv1.partition_broadcast(P)).then_inc(in_v1, DMA_DONE)
            act.dma_start(xT[:, :, HALF:TOKENS], x_feat[:, :, HALF:TOKENS]).then_inc(in_x2, DMA_DONE)
            act.dma_start(ids[:], token_ids.partition_broadcast(P)) \
                .then_inc(in_ids, DMA_DONE)
            for dst, src in ((wo1_sb, wo1), (wo2_sb, wo2), (a_sb, a_in)):
                act.dma_start(dst[:], src).then_inc(in_attn, DMA_DONE)
            act.dma_start(X[:], x_tok).then_inc(in_x, DMA_DONE)
            act.dma_start(bo1_sb[:], bo1.partition_broadcast(P)).then_inc(in_x, DMA_DONE)

            for step in PLAN:
                kind = step[0]
                if kind == "ST":
                    n = NTH[step]
                    filled(act, step)
                    if n > BUFFERS:
                        act.wait_ge(pv_done, n - BUFFERS)
                    release(act.activation(probs[:, (n - 1) % BUFFERS, :], slot_of(step)[:], ACT.Exp, scale=SM_SCALE), step)

                if kind == "PROJ" and step[1] == 1:
                    n = NTH[step]
                    filled(act, step)
                    act.wait_ge(parts_stored[step_at("PROJ", n - 2)], DMA_DONE)
                    act.activation(parts[:, n % 2, 0 if step[3] == "q" else PARTS - 1, :], slot_of(step)[:, 0:HALF],
                                   ACT.Copy).then_inc(one_ready, 1)
                if kind == "V" and step[1] == 1:
                    u = step[2]
                    last = ("PV", 1, 1, GROUPS - 1) if u else ("PV", 0, BATCHES - 1, GROUPS - 1)
                    filled(act, step)
                    act.wait_ge(v_cleared, 1)
                    act.wait_ge(pv_done, NTH[last])
                    release(act.activation(v[:, :, 0:HD], slot_of(step)[:, 0:HT * D] \
                                           .rearrange("p (n d) -> p n d", d=HD), ACT.Copy), step)
                if kind == "EVAC":
                    n = NTH[step]
                    act.wait_ge(pv_done, NTH["PV", step[1], step[2], 2 * step[3] + 1])
                    if n > 1:
                        act.wait_ge(turn_done, n - 1)
                    act.activation(o_sb[:], attn_out[:], ACT.Copy).then_inc(evac_done, 1)
                if kind == "YT":
                    n = NTH[step]
                    filled(act, step)
                    if n > 2:
                        a, b = divmod(n - 3, BATCHES)
                        filled(act, ("MOD" if a else "WO", a, b))
                    release(act.activation(yT[:, n % 2].rearrange("p k n -> p (k n)"), slot_of(step)[:, 0:HALF],
                                           ACT.Copy), step)
                if kind == "TR":
                    _, what, u = step
                    filled(act, step)
                    src = slot_of(step)
                    if what == "x1":
                        for k in range(KT):
                            ins = act.activation(x1_h[u][:, k, :], src[:, HALF * k:HALF * (k + 1)], ACT.Copy)
                            if k == 0:
                                ins.then_inc(x1_high, 1)
                    else:
                        act.wait_ge(in_attn2, 5 * DMA_DONE)
                        for k in (1, 0):
                            if k == 0:
                                act.wait_ge(bank_read_dve, u + 1)
                            ins = act.activation(xmT[:, k, cols_of(u)], src[:, HALF * k:HALF * (k + 1)], ACT.Copy,
                                                 scale=ln1_sb[:, k:k + 1])
                            if k == 1:
                                ins.then_inc(bank_read_act, 1)
                    release(ins, step)
                if kind == "SPLIT":
                    if step[1] == "ctx":
                        act.wait_ge(in_ctx, DMA_DONE)
                    elif step[1] == "w":
                        act.wait_ge(in_w[step[2]], DMA_DONE)
                        if step[2] < EARLY:
                            filled(act, ("V", 1, 1))
                        else:
                            filled(act, ("ST", 1, BATCHES - 1, GROUPS - 1))
                    src, high, _ = split_parts(step)
                    act.activation(high, src, ACT.Copy).then_inc(high_done, 1)
                if kind == "HID":
                    n = NTH[step]
                    width = 2 * HALF if step[1] == "moe" else HALF
                    filled(act, step)
                    if n > 2:
                        act.wait_ge(hidden_ready, n - 2)
                    act.activation(silu[:, n % 2, 0:width], slot_of(step)[:, 0:width], ACT.Silu) \
                        .then_inc(silu_ready, 1)
                if kind == "MOD":
                    filled(act, step)
                    if NTH[step] > 1:
                        act.wait_ge(mod_ready, NTH[step] - 1)
                    act.activation(tanh[:], slot_of(step)[0:COPIES * RANK, 0:SEQ], ACT.Tanh).then_inc(tanh_ready, 1)

        @block.vector
        def _(dve):
            link = chained(dve, dve_chain)
            def split(step):
                _, a, u, w, m = step
                n = NTH[step]
                rows = rows_of(step)
                src, rest, part = slot_of(step)[0:rows, 0:HALF], full[0:rows, n % 2, :], parts[0:rows, n % 2]
                filled(dve, step)
                if n == 1:
                    dve.wait_ge(in_rope, 3 * DMA_DONE)
                if a == 0:
                    bias = bq1_sb[:, m:m + 1] if w == "q" else bk1_sb[:, 0:1]
                    for j in range(HALF // SEQ):
                        c = slice(SEQ * j, SEQ * (j + 1))
                        ins = dve.scalar_tensor_tensor(out=rest[:, c], in0=src[:, c], scalar=bias,
                                                       in1=rope[0:rows, w == "k", :], op0=ALU.add, op1=ALU.mult)
                    release(ins, step)
                    released(dve, step)
                    src = rest
                if n > 2:
                    dve.wait_ge(parts_stored[step_at("PROJ", n - 2)], DMA_DONE)
                one, two, three = (part[:, i, :] for i in (range(PARTS) if w == "q" else reversed(range(PARTS))))
                if a == 0:
                    link(dve.tensor_copy(one, src))
                else:
                    dve.wait_ge(one_ready, n - step_count("PROJ", 0))
                ins = dve.tensor_tensor(rest, src, one, ALU.subtract)
                if a == 1:
                    release(ins, step)
                    released(dve, step)
                else:
                    link(ins)
                link(dve.tensor_copy(two, rest))
                dve.tensor_tensor(three, rest, two, ALU.subtract).then_inc(split_done, 1)

            def moments_of(step, tiles, eps, scale=None):
                for t in tiles:
                    ins = dve.bn_stats(stats[:, t, :], X[:, t, :])
                link(ins)
                for t in tiles:
                    ins = dve.bn_aggr(moments[:, t, :], stats[:, t, :])
                link(ins)
                s = slice(tiles[0], tiles[-1] + 1)
                dve.tensor_scalar(shifted[:, s], moments[:, s, 1], eps, None, ALU.add).then_inc(var_ready, 1)

            for step in PLAN:
                kind = step[0]
                if kind == "PROJ":
                    split(step)
                if kind == "V" and step[1] == 0:
                    u = step[2]
                    filled(dve, step)
                    dve.wait_ge(v_cleared, 1)
                    dve.wait_ge(in_v1, 2 * DMA_DONE)
                    four = "p (t h d) -> p t h d"
                    release(dve.tensor_tensor(
                        v1[:, HT * u:HT * (u + 1), :, 0:HD],
                        slot_of(step)[:, 0:HT * KV_HEADS * HD].rearrange(four, t=HT, d=HD),
                        bv1_sb[:].rearrange("p (t h d) -> p t h d", t=1, d=HD).broadcast_to([P, HT, KV_HEADS, HD]),
                        ALU.add), step)
                if kind == "S":
                    _, a, b, g = step
                    n = NTH["MAXT", a, b]
                    filled(dve, step)
                    if g == 0 and n > 2:
                        filled(dve, step_at("MAXT", n - 2))
                    src = slot_of(step)
                    h = GROUP * g
                    dve.tensor_reduce(neg_max[:, n % 2, HEADS + h:HEADS + h + GROUP],
                                      src[:, 0:GROUP * SEQ].rearrange("p (h k) -> p h k", h=GROUP), AX, ALU.max,
                                      negate=True)
                    ins = dve.tensor_reduce(neg_max[:, n % 2, h:h + GROUP],
                                            src[:, GROUP * SEQ:3 * HALF].rearrange("p (h k) -> p h k", h=GROUP),
                                            AX, ALU.max, negate=True)
                    release(ins, step)
                if kind == "MAXT":
                    n = NTH[step]
                    filled(dve, step)
                    if n > 2:
                        dve.wait_ge(max_stored, DMA_DONE * (n - 2))
                    src = slot_of(step)[0:2 * HEADS, 0:P]
                    m = max_parts[:, n % 2]
                    link(dve.tensor_copy(m[:, 0, :], src))
                    link(dve.tensor_tensor(max_rest[:], src, m[:, 0, :], ALU.subtract))
                    link(dve.tensor_copy(m[:, 1, :], max_rest[:]))
                    release(dve.tensor_tensor(m[:, 2, :], max_rest[:], m[:, 1, :], ALU.subtract), step)
                if kind == "TURN":
                    _, a, b, pair = step
                    n = NTH[step]
                    dve.wait_ge(turn_done, n)
                    if pair == 0 and (a, b) != (0, 0):
                        filled(dve, ("YT", a, b - 1) if b else ("YT", 0, BATCHES - 1))
                    src = turned_ps[:].rearrange("p (q h w) -> p q h w", q=2, w=VW)
                    link(dve.reciprocal(inv_sum[:], src[:, :, :, HD]))
                    w = 2 * GROUP * HD
                    dve.tensor_tensor(y[:, :, w * pair:w * (pair + 1)].rearrange("p q (h d) -> p q h d", d=HD),
                                      src[:, :, :, 0:HD],
                                      inv_sum[:].unsqueeze(3).broadcast_to([P, 2, 8, HD]), ALU.mult) \
                        .then_inc(y_ready, 1)
                if kind == "WO":
                    _, a, b = step
                    filled(dve, step)
                    dve.wait_ge(bias_added, 1)
                    release(dve.tensor_tensor(X[:, 2 * b:2 * b + 2, :], X[:, 2 * b:2 * b + 2, :],
                                              slot_of(step)[:, 0:2 * D].rearrange("p (t n) -> p t n", t=2),
                                              ALU.add), step)
                    released(dve, step)
                if kind == "RSTD":
                    _, what, i = step
                    tiles = norm_tiles(what, i)
                    if what == "ln1":
                        moments_of(step, tiles, LN_EPS)
                    else:
                        if what == "ln2":
                            dve.wait_ge(down_done, NTH["DOWN", "moe", i, EXPERTS - 1])
                        else:
                            if i % 2 == 0:
                                dve.wait_ge(pair_done, i // 2 + 1)
                            else:
                                dve.wait_ge(down_done, NTH["DOWN", "ffn", i // 2, FT - 1])
                            dve.wait_ge(x2_ready, i // 2 + 1)
                        for t in tiles[::2]:
                            xs = X[:, t:t + 2, :].rearrange("p t n -> p (t n)")
                            ins = dve.scalar_tensor_tensor(out=xs, in0=xs, scalar=1.0 if what == "ln2" else 2.0,
                                                           in1=accs[t // 2 % 2][:], op0=ALU.mult, op1=ALU.add)
                        ins.then_inc(z_ready, 1)
                        dve.wait_ge(z_ready, i + 1 + (HALVES if what == "ln3" else 0))
                        moments_of(step, tiles, LN_EPS)
                if kind == "NORM":
                    _, what, i = step
                    dve.wait_ge(rstd_ready, NTH[step])
                    if what == "ln2":
                        if i:
                            filled(dve, ("TR", "xn", i - 1))
                        else:
                            dve.wait_ge(masks_ready, 1)
                        for j, t in enumerate(norm_tiles(what, i)):
                            ins = dve.tensor_scalar(xn[:, j, :], X[:, t, :], moments[:, t, 0:1], rms[:, t:t + 1],
                                                    ALU.subtract, ALU.mult)
                        ins.then_inc(xn_ready, 1)
                        continue
                    for t in norm_tiles(what, i):
                        ins = dve.tensor_scalar(X[:, t, :], X[:, t, :], moments[:, t, 0:1], rstd[:, t:t + 1],
                                                ALU.subtract, ALU.mult)
                    ins.then_inc(norm_ready, 1)
                if kind == "TR":
                    _, what, u = step
                    filled(dve, step)
                    src = slot_of(step)
                    if what == "x1":
                        for k in range(KT):
                            if k == 0:
                                dve.wait_ge(x1_high, u + 1)
                            else:
                                released(dve, step, 1)
                            ins = dve.tensor_tensor(x1_l[u][:, k, :], src[:, HALF * k:HALF * (k + 1)],
                                                    x1_h[u][:, k, :].bitcast(F32), ALU.subtract)
                    else:
                        dve.wait_ge(in_attn2, 5 * DMA_DONE)
                        for k in (0, 1):
                            if k == 1:
                                dve.wait_ge(bank_read_act, u + 1)
                            ins = dve.tensor_scalar(xhT[:, k, cols_of(u)], src[:, HALF * k:HALF * (k + 1)],
                                                    ln2_sb[:, k:k + 1], None, ALU.mult)
                            if k == 0:
                                ins.then_inc(bank_read_dve, 1)
                    release(ins, step)
                if kind == "MULT":
                    _, what, u, i = step
                    step, n = ("HID", what, u, i), NTH[step]
                    if n > 2:
                        dve.wait_ge(down_done, n - 2)
                    width = 2 * HALF if what == "moe" else HALF
                    h = silu[:, n % 2, 0:width]
                    if what == "moe":
                        for f in range(2):
                            dve.wait_ge(masked_ready, 2 * n - 1 + f)
                            c = slice(HALF * f, HALF * (f + 1))
                            ins = dve.tensor_tensor(h[:, c], h[:, c], slot_of(step)[:, c], ALU.mult)
                    else:
                        dve.wait_ge(silu_ready, n)
                        ins = dve.tensor_tensor(h, h, slot_of(step)[:, HALF:2 * HALF], ALU.mult)
                    release(ins, step)
                    released(dve, step)
                    high, low = hidden_parts(what, n)
                    if step == ("HID", "ffn", 0, 0):
                        filled(dve, ("ST", 1, BATCHES - 1, GROUPS - 1))
                    link(dve.tensor_copy(high[:], h))
                    dve.tensor_tensor(low[:], h, high[:].bitcast(F32), ALU.subtract) \
                        .then_inc(hidden_ready, 1)
                if kind == "SPLIT":
                    dve.wait_ge(high_done, NTH[step])
                    src, high, low = split_parts(step)
                    if step[1] == "x":
                        filled(dve, ("MOD", 1, 2 * step[2] + 1))
                    dve.tensor_tensor(low, src, high.bitcast(F32), ALU.subtract).then_inc(low_done, 1)
                if kind == "SPLIT_B":
                    dve.wait_ge(in_b, COPIES * DMA_DONE)
                    link(dve.tensor_copy(b3[:], b_raw[:]))
                    last = slice((COPIES - 1) * RANK, COPIES * RANK)
                    dve.tensor_tensor(b3[last, :], b_raw[last, :], b3[last, :].bitcast(F32), ALU.subtract) \
                        .then_inc(b_ready, 1)
                if kind == "MOD":
                    _, a, b = step
                    dve.wait_ge(tanh_ready, NTH[step])
                    release(dve.scalar_tensor_tensor(out=tanh[:], in0=tanh[:], scalar=MOD_SCALE,
                                                     in1=slot_of(step)[0:COPIES * RANK, HALF:HALF + SEQ],
                                                     op0=ALU.mult, op1=ALU.mult), step)
                    released(dve, step)
                    m = modT[:, SEQ * b:SEQ * (b + 1)]
                    link(dve.tensor_copy(m, tanh[:]))
                    dve.tensor_tensor(m[0:RANK], tanh[0:RANK, :], m[0:RANK].bitcast(F32), ALU.subtract) \
                        .then_inc(mod_ready, 1)
                if kind == "WOA":
                    filled(dve, step)
                    release(dve.tensor_copy(woa_sb[:].rearrange("p k r -> p (k r)"),
                                            slot_of(step)[:, 0:KT * COPIES * RANK]), step)

        @block.tensor
        def _(pe):
            mm = pe.matmul

            def split_mm(dst, operands, start=True, stop=True):
                passes = [(a, b) for a_h, a_l, b_h, b_l in operands for a, b in ((a_h, b_h), (a_h, b_l), (a_l, b_h))]
                for j, (a, b) in enumerate(passes):
                    ins = mm(dst, a, b, start=start and j == 0, stop=stop and j == len(passes) - 1,
                             skip_group_check=True)
                return ins

            def take(step):
                slot, _, before = RING_AT[step]
                if before:
                    pe.wait_ge(slot_free[slot], before)
                return slots[slot]

            def give(ins, step):
                ins.then_inc(slot_full[RING_AT[step][0]], 1)

            def project(step):
                _, a, u, w, m = step
                dst = take(step)
                rows = rows_of(step)
                if a == 0:
                    pe.wait_ge(in_k1, 2 * DMA_DONE)
                    if w == "q":
                        pe.wait_ge(in_q1, DMA_DONE)
                    if u:
                        pe.wait_ge(in_x2, DMA_DONE)
                    x, weights = xT, wq1_sb if w == "q" else wk1_sb
                else:
                    released(pe, ("TR", "xn", u))
                    pe.wait_ge(in_attn2, 5 * DMA_DONE)
                    x, weights = xmT, wq2_sb if w == "q" else wk2_sb
                for k in range(KT):
                    ins = mm(dst[0:rows, 0:HALF], weights[:, k, P * m:P * m + rows], x[:, k, cols_of(u)],
                             start=k == 0, stop=k == KT - 1)
                give(ins, step)

            def values(step):
                _, a, u = step
                dst = take(step)
                x, weights, w = (xmT, wv2_sb, D) if a else (xT, wv1_sb, KV_HEADS * HD)
                if a == 0:
                    pe.wait_ge(in_v1, 2 * DMA_DONE)
                    if u:
                        pe.wait_ge(in_x2, DMA_DONE)
                for t in range(HT):
                    for k in range(KT):
                        c = HALF * u + P * t
                        ins = mm(dst[:, w * t:w * (t + 1)], x[:, k, c:c + P], weights[:, k, :],
                                 start=k == 0, stop=k == KT - 1)
                give(ins, step)

            def kv(a, h):
                return h if a else h // (HEADS // KV_HEADS)

            def scores(step):
                _, a, b, g = step
                dst = take(step)
                for w, m in (("q", g // 2), ("k", g // 2 if a else 0)):
                    pe.wait_ge(stacked["PROJ", a, b // 2, w, m], DMA_DONE * len(RUNS))
                if g == 0 and b == 0 and a == 0:
                    pe.wait_ge(consts_ready, 1)
                u, c = b // 2, SEQ * (b % 2)
                group = dict(stop=False, skip_group_check=True)
                for j in range(GROUP):
                    h = GROUP * g + j
                    mm(dst[:, SEQ * j:SEQ * (j + 1)], qs[0:STACK, u, h, c + P:c + SEQ],
                       ks[0:STACK, u, kv(a, h), c:c + SEQ],
                       start=j % 2 == 0, **group)
                for j in range(GROUP):
                    h = GROUP * g + j
                    at = GROUP * SEQ + P * j
                    mm(dst[:, at:at + P], qs[0:STACK, u, h, c:c + P], ks[0:STACK, u, kv(a, h), c:c + P],
                       start=j == 0, **group)
                for j in range(0, GROUP, 2):
                    mm(dst[:, SEQ * j:SEQ * (j + 2)].rearrange("p (h k) -> p h k", h=2)[:, :, P:SEQ], ident16[:],
                       causal_q[:, 0:2, :], start=False, stop=True, skip_group_check=True)
                ins = mm(dst[:, GROUP * SEQ:3 * HALF], ident16[:], causal_q[:].rearrange("p h k -> p (h k)"),
                         start=False, stop=True, skip_group_check=True)
                give(ins, step)

            def turn_maxima(step):
                n = NTH[step]
                dst = take(step)
                released(pe, ("S", step[1], step[2], GROUPS - 1))
                give(pe.transpose(dst[0:2 * HEADS, 0:P], neg_max[:, n % 2, :], ident[:]), step)

            def scores_turned(step):
                _, a, b, g = step
                dst = take(step)
                pe.wait_ge(max_stacked["MAXT", a, b], 2 * DMA_DONE)
                if g == 0 and b == 0 and a == 0:
                    pe.wait_ge(ones_ready, 1)
                u, c, rows = b // 2, SEQ * (b % 2), STACK + PARTS
                group = dict(stop=False, skip_group_check=True)
                early, late = dst[:, 0:GROUP * SEQ], dst[:, GROUP * SEQ:3 * HALF]
                per = 1 if a else 2
                for j in range(0, GROUP, per):
                    h = GROUP * g + j
                    mm(early[:, SEQ * j:SEQ * (j + per)], ks[0:rows, u, kv(a, h), c:c + P],
                       qs[0:rows, u, h:h + per, c:c + SEQ], start=j % 2 == 0, **group)
                per = 1 if a else GROUP
                for j in range(0, GROUP, per):
                    h = GROUP * g + j
                    mm(late[:, P * j:P * (j + per)], ks[0:rows, u, kv(a, h), c + P:c + SEQ],
                       qs[0:rows, u, h:h + per, c + P:c + SEQ], start=j == 0, **group)
                for j in range(0, GROUP, 2):
                    mm(early[:, SEQ * j:SEQ * (j + 2)].rearrange("p (h q) -> p h q", h=2)[:, :, 0:P], ident16[:],
                       causal_k[:, 0:2, :], start=False, stop=True, skip_group_check=True)
                ins = mm(late, ident16[:], causal_k[:].rearrange("p h q -> p (h q)"),
                         start=False, stop=True, skip_group_check=True)
                give(ins, step)

            def weigh_values(step):
                _, a, b, g = step
                n = NTH["ST", a, b, g]
                released(pe, ("ST", a, b, g))
                if g == 0:
                    released(pe, ("V", a, b // 2))
                if g % 2 == 0:
                    done = NTH["EVAC", a, b, g // 2] - 1
                    if done:
                        pe.wait_ge(evac_done, done)
                    if (a, b, g) == (1, 0, 0):
                        pe.wait_ge(z_ready, HALVES)
                e = probs[:, (n - 1) % BUFFERS, :]
                early = e[:, 0:GROUP * SEQ].rearrange("p (h q) -> p h q", h=GROUP)
                late = e[:, GROUP * SEQ:3 * HALF].rearrange("p (h q) -> p h q", h=GROUP)
                at = SEQ * (g % 2)
                for kt in range(2):
                    for j in range(GROUP):
                        vt = (v2[:, 2 * (b % 2) + kt, GROUP * g + j, :] if a else v1[:, 2 * b + kt, g, :])
                        ins = mm(attn_out[VW * j:VW * (j + 1), at + P * kt:at + SEQ], vt,
                                 late[:, j, :] if kt else early[:, j, :],
                                 start=kt == 0 and g % 2 == 0, stop=kt == 1, skip_group_check=True,
                                 tile_position=(0, VW * j))
                ins.then_inc(pv_done, 1)

            def turn_outputs(step):
                n = NTH[step]
                pe.wait_ge(evac_done, n)
                if n > 1:
                    pe.wait_ge(y_ready, n - 1)
                for qt in range(2):
                    for gg in range(2):
                        src = SEQ * gg + P * qt
                        dst = P * (2 * qt + gg)
                        ins = pe.transpose(turned_ps[:, dst:dst + P], o_sb[:, src:src + P], ident[:])
                ins.then_inc(turn_done, 1)

            def turn_y(step):
                _, a, b = step
                dst = take(step)
                pe.wait_ge(y_ready, NTH["TURN", a, b, 1])
                for k in range(KT):
                    for qt in range(2):
                        at = SEQ * k + P * qt
                        ins = pe.transpose(dst[:, at:at + P], y[:, qt, P * k:P * (k + 1)], ident[:])
                give(ins, step)

            def output_product(step):
                _, a, b = step
                dst = take(step)
                n = NTH["YT", a, b]
                released(pe, ("YT", a, b))
                pe.wait_ge(in_attn, 3 * DMA_DONE)
                for qt in range(2):
                    for k in range(KT):
                        ins = mm(dst[:, D * qt:D * (qt + 1)], yT[:, n % 2, k, P * qt:P * (qt + 1)], wo1_sb[:, k, :],
                                 start=k == 0, stop=k == KT - 1)
                give(ins, step)

            def modulation(step):
                _, a, b = step
                dst = take(step)
                n = NTH["YT", a, b]
                for k in range(KT):
                    mm(dst[0:COPIES * RANK, HALF:HALF + SEQ], a_sb[:, k, :], xhT[:, k, SEQ * b:SEQ * (b + 1)],
                       start=k == 0, stop=k == KT - 1)
                released(pe, ("YT", a, b))
                released(pe, ("WOA",))
                for k in range(KT):
                    ins = mm(dst[0:COPIES * RANK, 0:SEQ], woa_sb[:, k, :], yT[:, n % 2, k, :],
                             start=k == 0, stop=k == KT - 1)
                give(ins, step)

            def fold(step):
                dst = take(step)
                pe.wait_ge(in_attn, 3 * DMA_DONE)
                for m in range(KT):
                    for k in range(KT):
                        ins = mm(dst[:, COPIES * RANK * m:COPIES * RANK * (m + 1)], wo2_sb[:, k, P * m:P * (m + 1)], a_sb[:, k, :],
                                 start=k == 0, stop=k == KT - 1)
                give(ins, step)

            def turn_tokens(step):
                _, what, u = step
                dst = take(step)
                if what == "x1":
                    pe.wait_ge(norm_ready, NTH["NORM", "ln1", 2 * u + 1])
                else:
                    pe.wait_ge(xn_ready, u + 1)
                for k in range(KT):
                    for t in range(HT):
                        src = (X[:, HT * u + t] if what == "x1" else xn[:, t])[:, P * k:P * (k + 1)]
                        at = HALF * k + P * t
                        ins = pe.transpose(dst[:, at:at + P], src, ident[:])
                give(ins, step)

            def hidden_products(step):
                _, what, u, i = step
                dst = take(step)
                if what == "moe":
                    if i == 0:
                        released(pe, ("TR", "x1", u))
                    pe.wait_ge(low_done, NTH["SPLIT", "ctx", i])
                    for f in range(2):
                        ins = split_mm(dst[:, HALF * f:HALF * (f + 1)],
                                       [(ctx_h[:, KT * i + k, P * f:P * (f + 1)], ctx_l[:, KT * i + k, P * f:P * (f + 1)],
                                         x1_h[u][:, k, :], x1_l[u][:, k, :]) for k in range(KT)])
                else:
                    if i == 0:
                        pe.wait_ge(mod_ready, NTH["MOD", 1, 2 * u + 1])
                        pe.wait_ge(b_ready, 1)
                    if u == 0:
                        pe.wait_ge(low_done, NTH["SPLIT", "w", i])
                    elif i == 0:
                        pe.wait_ge(low_done, NTH["SPLIT", "x", 1])
                    c = cols_of(u)
                    for half, side in enumerate((0, KT * P)):
                        if half == 0:
                            mm(dst[:, 0:HALF], b3[:, P * i:P * (i + 1)], modT[:, c], start=True, stop=False,
                               skip_group_check=True)
                        ins = split_mm(dst[:, HALF * half:HALF * (half + 1)],
                                       [(w_h[i][:, side + P * k:side + P * (k + 1)],
                                         w_l[:, i, side + P * k:side + P * (k + 1)],
                                         xh_h[:, k, c], xh_l[:, k, c]) for k in range(KT)], start=half == 1)
                give(ins, step)

            def down_product(step):
                _, what, u, i = step
                n = NTH["HID", what, u, i]
                pe.wait_ge(hidden_ready, n)
                if i == 0:
                    if what == "moe":
                        if u == 0:
                            pe.wait_ge(evac_done, NTH["EVAC", 0, BATCHES - 1, 1])
                            pe.wait_ge(y_ready, NTH["TURN", 0, BATCHES - 1, 1])
                        else:
                            pe.wait_ge(z_ready, 1)
                    elif u == 0:
                        pe.wait_ge(evac_done, NTH["EVAC", 1, BATCHES - 1, 1])
                        pe.wait_ge(y_ready, NTH["TURN", 1, BATCHES - 1, 1])
                    else:
                        pe.wait_ge(z_ready, HALVES + 2)
                ktiles, last = (2, EXPERTS - 1) if what == "moe" else (1, FT - 1)
                high, low = hidden_parts(what, n)
                for k in range(ktiles):
                    for t in range(HT):
                        at = HALF * k + P * t
                        if what == "moe":
                            rhs = ctx_h[:, ktiles * i + k, :], ctx_l[:, ktiles * i + k, :]
                        else:
                            rhs = w_h[i][:, 2 * D:WIDE], w_l[:, i, 2 * D:WIDE]
                        ins = split_mm(accs[t // 2][:, D * (t % 2):D * (t % 2 + 1)],
                                       [(high[:, at:at + P], low[:, at:at + P], *rhs)],
                                       start=i == 0 and k == 0 and t % 2 == 0, stop=i == last and k == ktiles - 1)
                        if what == "ffn" and i == last and t == 1:
                            ins.then_inc(pair_done, 1)
                ins.then_inc(down_done, 1)

            parts_of = {"PROJ": project, "V": values, "S": scores, "MAXT": turn_maxima, "ST": scores_turned,
                        "PV": weigh_values, "TURN": turn_outputs, "YT": turn_y, "WO": output_product,
                        "MOD": modulation, "WOA": fold, "TR": turn_tokens, "HID": hidden_products,
                        "DOWN": down_product}
            for step in PLAN:
                if step[0] in parts_of:
                    parts_of[step[0]](step)


def rope_tables():
    inv = np.float32(10000.0) ** (np.float32(-2.0) * np.arange(HD // 2, dtype=np.float32) / np.float32(HD))
    theta = np.arange(SEQ, dtype=np.float32)[:, None] * inv[None, :].astype(np.float32)
    table = (np.cos(theta) + np.sin(theta)).T.astype(np.float32)
    tables = np.zeros((P, 2, SEQ), np.float32)
    tables[:, 0] = np.repeat(np.tile(table, (2, 1)), P // HD, axis=0)
    tables[0:KV_HEADS * HD, 1] = np.repeat(np.tile(table, (2, 1)), KV_HEADS, axis=0)
    return tables


def kernel(**inputs):
    import concourse.bacc as bacc
    from concourse.bass_utils import run_bass_kernel_spmd

    g = {n: np.asarray(a) for n, a in inputs.items()}

    def by_place(a):
        heads = min(P, a.shape[0]) // HD
        return a.reshape(-1, heads, HD, *a.shape[1:]).swapaxes(1, 2).reshape(a.shape)

    def weight(name, order=lambda a: a):
        w = order(g[name])
        return w.T.reshape(-1, P, w.shape[0]).transpose(1, 0, 2)

    def columns(a):
        return a.reshape(-1, P).T

    def by_hidden_tile(name):
        return weight(name).reshape(P, KT, FT, P).transpose(0, 2, 1, 3).reshape(P, FT, KT * P)

    x = g["x"].reshape(TOKENS, D)
    arrays = {
        "x_tok": x.reshape(TILES, P, D).transpose(1, 0, 2),
        "x_feat": x.T.reshape(KT, P, TOKENS).transpose(1, 0, 2),
        "token_ids": g["itok_BxS_13_99985"].reshape(TOKENS),
        "ctx_t": g["ctx_2048"].transpose(0, 2, 1).reshape(EXPERTS * KT, P, EF).transpose(1, 0, 2),
        "wq1": weight("L0_attn_Wq", by_place), "bq1": columns(by_place(g["L0_attn_bq"])),
        "wk1": weight("L0_attn_Wk", by_place), "bk1": by_place(g["L0_attn_bk"]).reshape(-1, 1),
        "wv1": weight("L0_attn_Wv"), "bv1": g["L0_attn_bv"],
        "wo1": weight("L0_attn_Wo"), "bo1": g["L0_attn_bo"],
        "ln1": columns(g["L0_ffn_ln1_w"]), "ln2": columns(g["L0_ffn_ln2_w"]),
        "wq2": weight("L0_ffn_Wq", by_place), "wk2": weight("L0_ffn_Wk", by_place), "wv2": weight("L0_ffn_Wv"),
        "wo2": g["L0_ffn_Wo"].reshape(KT, P, D).transpose(1, 0, 2),
        "a_in": np.tile(g["L0_ffn_A"].reshape(KT, P, RANK).transpose(1, 0, 2), (1, 1, COPIES)),
        "b_in": g["L0_ffn_B"],
        "w_ffn": np.concatenate([by_hidden_tile("L0_ffn_W_in_base"), by_hidden_tile("L0_ffn_W_up_base"),
                                 weight("L0_ffn_W_down")], axis=2),
        "rope_in": rope_tables(),
    }
    nc = bacc.Bacc("TRN2", target_bir_lowering=False, num_devices=1)
    args = []
    for name, a in arrays.items():
        a = arrays[name] = np.ascontiguousarray(a)
        args.append(nc.dram_tensor(name, a.shape, mybir.dt.from_np(a.dtype), kind="ExternalInput").ap())
    args.append(nc.dram_tensor("out", (P, TILES, D), F32, kind="ExternalOutput").ap())
    decoder_layer(nc, *args)
    got = run_bass_kernel_spmd(nc, [arrays], core_ids=[0]).results[0]["out"]
    return np.ascontiguousarray(got.transpose(1, 0, 2)).reshape(BATCHES, SEQ, D)
```

```python
from contextlib import ExitStack

import numpy as np

import concourse.bass as bass
from concourse import mybir

P = 128
BATCHES, SEQ, D = 4, 256, 256
TOKENS = BATCHES * SEQ
TILES = TOKENS // P
HALF = 512
HALVES = TOKENS // HALF
HT = HALF // P
KT = D // P
HEADS, HD = 16, 16
KV_HEADS = 4
GROUP = 4
GROUPS = HEADS // GROUP
VW = 32
EXPERTS, EF = 4, 256
TOKENS_PER_EXPERT = 12500 // EXPERTS
FF = 1024
FT = FF // P
RANK = 16
MOD_SCALE = 0.1
LN_EPS, RMS_EPS = 1e-5, 1e-6
SM_SCALE = HD ** -0.5
MASKED = -1e30
PARTS = 3
RUNS = [3, 2, 1]
STACK = HD * sum(RUNS)
BLOCK = 64
MASK_ROWS = SEQ // BLOCK - 1
MAX_ROW = STACK + MASK_ROWS
BUFFERS = 3
EARLY = 2
DMA_DONE = 16
COPIES = 3
WIDE = 3 * D

F32, F32R, BF16, I32 = mybir.dt.float32, mybir.dt.float32r, mybir.dt.bfloat16, mybir.dt.int32
ALU = mybir.AluOpType
ACT = mybir.ActivationFunctionType
AX, AXY = mybir.AxisListType.X, mybir.AxisListType.XY

RING = {"PROJ": 1, "V": 1, "S": 2, "MAXT": 1, "ST": 2, "YT": 1, "WO": 1, "TR": 2, "HID": 1, "MOD": 1,
        "WOA": 1}


ORDER = """
    # attention 1: projections, and the maxima of the first batches
    PROJ 0 0 k 0; PROJ 0 0 q 0; PROJ 0 0 q 1; V 0 0; PROJ 0 1 k 0; PROJ 0 1 q 0; V 0 1; S 0 0 0; S 0 0 1;
    S 0 0 2; S 0 0 3; MAXT 0 0; S 0 1 0; S 0 1 1; PROJ 0 1 q 1;
    # attention 1: the loop over groups
    ST 0 0 0; ST 0 0 1; S 0 1 2; S 0 1 3; PV 0 0 0; S 0 2 0; MAXT 0 1; PV 0 0 1; EVAC 0 0 0; WOA; ST 0 0 2;
    S 0 2 1; S 0 2 2; ST 0 0 3; TURN 0 0 0; PV 0 0 2; ST 0 1 0; PV 0 0 3; EVAC 0 0 1; SPLIT ctx 0;
    ST 0 1 1; S 0 2 3; ST 0 1 2; TURN 0 0 1; S 0 3 0; PV 0 1 0; PV 0 1 1; YT 0 0; MAXT 0 2; WO 0 0;
    EVAC 0 1 0; SPLIT ctx 1; S 0 3 1; S 0 3 2; PV 0 1 2; ST 0 1 3; ST 0 2 0; ST 0 2 1; RSTD ln1 0;
    TURN 0 1 0; NORM ln1 0; PV 0 1 3; EVAC 0 1 1; S 0 3 3; SPLIT ctx 2; SPLIT ctx 3; TURN 0 1 1; PV 0 2 0;
    MAXT 0 3; PV 0 2 1; YT 0 1; ST 0 2 2; WO 0 1; RSTD ln1 1; EVAC 0 2 0; TURN 0 2 0; ST 0 2 3; ST 0 3 0;
    PV 0 2 2; PV 0 2 3; EVAC 0 2 1; NORM ln1 1; ST 0 3 1; TURN 0 2 1; TR x1 0; PV 0 3 0; YT 0 2; PV 0 3 1;
    EVAC 0 3 0; ST 0 3 2; TURN 0 3 0; ST 0 3 3; WO 0 2; PV 0 3 2; PV 0 3 3; EVAC 0 3 1; RSTD ln1 2;
    TURN 0 3 1; YT 0 3;
    # experts, first half
    HID moe 0 0; NORM ln1 2; MULT moe 0 0; HID moe 0 1; MULT moe 0 1; WO 0 3; RSTD ln1 3; HID moe 0 2;
    NORM ln1 3; MULT moe 0 2; DOWN moe 0 0; DOWN moe 0 1; TR x1 1; HID moe 0 3;
    # experts, second half; normalisation, and attention 2 begins
    HID moe 1 0; MULT moe 0 3; MULT moe 1 0; DOWN moe 0 2; HID moe 1 1; DOWN moe 0 3; RSTD ln2 0;
    DOWN moe 1 0; HID moe 1 2; MULT moe 1 1; NORM ln2 0; TR xn 0; DOWN moe 1 1; MULT moe 1 2; PROJ 1 0 k 0;
    PROJ 1 0 q 0; HID moe 1 3; MULT moe 1 3; DOWN moe 1 2; PROJ 1 0 k 1; PROJ 1 0 q 1; DOWN moe 1 3;
    RSTD ln2 1; V 1 0; S 1 0 0; S 1 0 1; NORM ln2 1; S 1 0 2; S 1 0 3; TR xn 1; S 1 1 0; MAXT 1 0; S 1 1 1;
    RESIDUAL 0; PROJ 1 1 k 0; PROJ 1 1 q 0;
    # attention 2: the loop over groups
    ST 1 0 0; S 1 1 2; PROJ 1 1 k 1; PROJ 1 1 q 1; ST 1 0 1; S 1 1 3; RESIDUAL 1; ST 1 0 2; PV 1 0 0;
    PV 1 0 1; EVAC 1 0 0; MAXT 1 1; S 1 2 0; S 1 2 1; TURN 1 0 0; PV 1 0 2; ST 1 0 3; S 1 2 2; S 1 2 3;
    PV 1 0 3; EVAC 1 0 1; ST 1 1 0; TURN 1 0 1; S 1 3 0; ST 1 1 1; PV 1 1 0; MAXT 1 2; ST 1 1 2; PV 1 1 1;
    YT 1 0; S 1 3 1; EVAC 1 1 0; MOD 1 0; TURN 1 1 0; ST 1 1 3; ST 1 2 0; PV 1 1 2; PV 1 1 3; EVAC 1 1 1;
    S 1 3 2; V 1 1; TURN 1 1 1; S 1 3 3; ST 1 2 1; PV 1 2 0; YT 1 1; MAXT 1 3; PV 1 2 1; EVAC 1 2 0;
    ST 1 2 2; ST 1 2 3; TURN 1 2 0; MOD 1 1; SPLIT x 0; PV 1 2 2; ST 1 3 0; PV 1 2 3; EVAC 1 2 1; SPLIT_B;
    ST 1 3 1; ST 1 3 2; TURN 1 2 1; PV 1 3 0; PV 1 3 1; EVAC 1 3 0; YT 1 2; SPLIT w 0; ST 1 3 3; MOD 1 2;
    SPLIT w 1; SPLIT w 2; PV 1 3 2; PV 1 3 3; TURN 1 3 0; EVAC 1 3 1;
    # FFN, first half
    HID ffn 0 0; TURN 1 3 1; MULT ffn 0 0; HID ffn 0 1; MULT ffn 0 1; SPLIT w 3; YT 1 3; DOWN ffn 0 0;
    MOD 1 3; SPLIT w 4; HID ffn 0 2; MULT ffn 0 2; HID ffn 0 3; DOWN ffn 0 1; DOWN ffn 0 2; MULT ffn 0 3;
    SPLIT w 5; SPLIT w 6; HID ffn 0 4; HID ffn 0 5; MULT ffn 0 4; SPLIT x 1; SPLIT w 7; DOWN ffn 0 3;
    DOWN ffn 0 4; HID ffn 0 6; HID ffn 0 7; MULT ffn 0 5; DOWN ffn 0 5; MULT ffn 0 6; MULT ffn 0 7;
    # FFN, second half, and the results
    HID ffn 1 0; DOWN ffn 0 6; DOWN ffn 0 7; MULT ffn 1 0; RSTD ln3 0; RSTD ln3 1; NORM ln3 0; OUT ln3 0;
    HID ffn 1 1; HID ffn 1 2; NORM ln3 1; MULT ffn 1 1; DOWN ffn 1 0; HID ffn 1 3; MULT ffn 1 2;
    MULT ffn 1 3; DOWN ffn 1 1; DOWN ffn 1 2; HID ffn 1 4; MULT ffn 1 4; HID ffn 1 5; DOWN ffn 1 3;
    DOWN ffn 1 4; MULT ffn 1 5; HID ffn 1 6; MULT ffn 1 6; HID ffn 1 7; MULT ffn 1 7; DOWN ffn 1 5;
    DOWN ffn 1 6; DOWN ffn 1 7; RSTD ln3 2; RSTD ln3 3; NORM ln3 2; NORM ln3 3; OUT ln3 1; OUT ln3 2;
    OUT ln3 3;
"""


def make_plan():
    lines = [line for line in ORDER.splitlines() if not line.strip().startswith("#")]
    steps = [step.split() for step in " ".join(lines).split(";") if step.strip()]
    return [tuple(int(w) if w.isdigit() else w for w in step) for step in steps]


PLAN = make_plan()


def count_steps():
    nth, ring, tail, seen, filled, released, last = {}, {}, {}, {}, [0, 0], [0, 0], [None, None]
    for step in PLAN:
        kind = step[0]
        seen[kind] = seen.get(kind, 0) + 1
        nth[step] = seen[kind]
        if kind in RING:
            slot = sum(filled) % 2
            filled[slot] += 1
            ring[step] = (slot, filled[slot], released[slot])
            tail[step] = int(kind in ("S", "ST") and last[slot] in ("S", "ST"))
            released[slot] += RING[kind]
            last[slot] = kind
    return nth, ring, tail


NTH, RING_AT, TAIL = count_steps()


def step_at(kind, n):
    return [s for s in PLAN if s[0] == kind][n - 1]


def rows_of(step):
    return KV_HEADS * HD if step[1] == 0 and step[3] == "k" else P


def step_count(kind, a):
    return sum(s[:2] == (kind, a) for s in PLAN)


def decoder_layer(nc, x_tok, x_feat, token_ids, ctx_t, wq1, bq1, wk1, bk1, wv1, bv1, wo1, bo1, ln1, ln2,
                  wq2, wk2, wv2, wo2, a_in, b_in, w_ffn, rope_in, mask_rows, out):
    with ExitStack() as ctx:
        def sb(name, shape, dt=F32):
            return ctx.enter_context(nc.sbuf_tensor(name, shape, dt))

        def psum(name, shape):
            return ctx.enter_context(nc.psum_tensor(name, shape, F32))

        starts = {}

        def sb_region(name, shape, dt=F32):
            t = sb(name, shape, dt)
            starts[name] = nc.sbuf_base - int(np.prod(shape[1:])) * mybir.dt.size(dt)
            return t

        def over(region, at, name, shape, dt=F32R):
            return nc.alloc_sbuf_tensor_at(name, shape, dt, offset=starts[region] + at)

        def sem(name):
            return ctx.enter_context(nc.semaphore(name))

        def dram(name, shape, dt):
            return nc.dram_tensor(name, shape, dt, kind="Internal").ap()

        slots = [psum(f"slot{i}", [P, 3 * HALF]) for i in range(2)]
        attn_out = psum("attn_out", [P, HALF])
        turned_ps = psum("turned_ps", [P, HALF])
        accs = [attn_out, turned_ps]

        xT = sb_region("xT", [P, KT, TOKENS])
        X = sb("X", [P, TILES, D])
        xn = sb("xn", [P, HT, D])
        ids = xn[:].rearrange("p t n -> p (t n)").bitcast(I32)
        xmT = sb_region("xmT", [P, KT, TOKENS])
        xhT = sb_region("xhT", [P, KT, TOKENS])
        full = sb("full", [P, 2, HALF])
        parts = sb("parts", [P, 2, PARTS, HALF], BF16)
        qs = sb_region("qs", [P, HALVES, HEADS, HALF], BF16)
        ks = sb_region("ks", [P, HALVES, HEADS, HALF], BF16)
        probs = sb_region("probs", [P, BUFFERS, 3 * HALF])
        silu = probs[:].rearrange("p b n -> p (b n)")[:, 0:4 * HALF].rearrange("p (s n) -> p s n", s=2)
        v = sb("v", [P, TILES * KV_HEADS * 2, VW])
        v1 = v[:, 0:TILES * KV_HEADS, :].rearrange("p (t h) w -> p t h w", t=TILES)
        v2 = v[:, :, :].rearrange("p (t h) w -> p t h w", t=HT)
        o_sb = sb_region("o_sb", [P, HALF])
        y = sb("y", [P, 2, D])
        yT = sb_region("yT", [P, 2, KT, SEQ])
        masks = sb_region("masks", [P, EXPERTS, TOKENS], BF16)
        neg_max = sb("neg_max", [P, 2, 2 * HEADS])
        max_rest = sb("max_rest", [2 * HEADS, P])
        max_parts = sb("max_parts", [2 * HEADS, 2, PARTS, P], BF16)
        tanh = sb("tanh", [COPIES * RANK, SEQ])
        modT = sb("modT", [COPIES * RANK, TOKENS], F32R)
        inv_sum = sb("inv_sum", [P, 2, 8])
        stats = sb("stats", [P, TILES, 6])
        moments = sb("moments", [P, TILES, 2])
        shifted = sb("shifted", [P, TILES])
        rstd = sb("rstd", [P, TILES])
        rms = sb("rms", [P, TILES])
        minus_half = sb("minus_half", [P, TILES])

        wq1_sb, wk1_sb = sb("wq1_sb", [P, KT, D]), sb("wk1_sb", [P, KT, KV_HEADS * HD])
        wv1_sb, wo1_sb = sb("wv1_sb", [P, KT, KV_HEADS * HD]), sb("wo1_sb", [P, KT, D])
        bq1_sb, bk1_sb = sb("bq1_sb", [P, KT]), sb("bk1_sb", [KV_HEADS * HD, 1])
        bv1_sb, bo1_sb = sb("bv1_sb", [P, KV_HEADS * HD]), sb("bo1_sb", [P, D])
        ln1_sb, ln2_sb = sb("ln1_sb", [P, KT]), sb("ln2_sb", [P, KT])
        ctx_sb = sb_region("ctx_sb", [P, EXPERTS * KT, EF])
        ctx_h = sb("ctx_h", [P, EXPERTS * KT, EF], F32R)
        ctx_l = sb("ctx_l", [P, EXPERTS * KT, EF], F32R)
        wq2_sb, wk2_sb = sb("wq2_sb", [P, KT, D]), sb("wk2_sb", [P, KT, D])
        wv2_sb, wo2_sb = sb("wv2_sb", [P, KT, D]), sb("wo2_sb", [P, KT, D])
        a_sb, woa_sb = sb("a_sb", [P, KT, COPIES * RANK]), sb("woa_sb", [P, KT, COPIES * RANK])
        b3 = sb("b3", [COPIES * RANK, FF], F32R)
        rope = sb("rope", [P, 2, SEQ])
        ident, ident16 = sb("ident", [P, P]), sb("ident16", [P, P], BF16)
        causal_q, causal_k = sb("causal_q", [P, GROUP, BLOCK], BF16), sb("causal_k", [P, GROUP, BLOCK], BF16)

        kb = 1024
        x1_h = [over("xhT", 0, "x1_h0", [P, KT, HALF]), over("o_sb", 0, "x1_h1", [P, KT, HALF])]
        x1_l = [over("xhT", 4 * kb, "x1_l0", [P, KT, HALF]), over("yT", 0, "x1_l1", [P, KT, HALF])]
        hidden_h = [over("xT", 0, "hidden_h0", [P, 2 * HALF]), over("probs", 8 * kb, "hidden_h1", [P, 2 * HALF])]
        hidden_l = [over("xT", 4 * kb, "hidden_l0", [P, 2 * HALF]), over("probs", 12 * kb, "hidden_l1", [P, 2 * HALF])]
        w_raw = over("ctx_sb", 0, "w_raw", [P, FT, WIDE], F32)
        b_raw = over("masks", 0, "b_raw", [COPIES * RANK, FF], F32)
        w_l = over("ctx_sb", 0, "w_l", [P, FT, WIDE])
        w_early, w_late = over("xmT", 0, "w_early", [P, EARLY, WIDE]), over("ks", 0, "w_late", [P, FT - EARLY, WIDE])
        w_h = [w_early[:, f, :] if f < EARLY else w_late[:, f - EARLY, :] for f in range(FT)]
        xh_h, xh_l = over("xT", 0, "xh_h", [P, KT, TOKENS]), over("xhT", 0, "xh_l", [P, KT, TOKENS])
        ffn_hidden_h = [over("qs", 4 * kb * i, f"ffn_hidden_h{i}", [P, HALF]) for i in range(2)]
        ffn_hidden_l = [over("qs", 4 * kb * i + 2 * kb, f"ffn_hidden_l{i}", [P, HALF]) for i in range(2)]

        scratch = {s: dram("scratch_" + "_".join(map(str, s[1:])), (PARTS, rows_of(s), HALF), BF16)
                   for s in PLAN if s[0] == "PROJ"}
        m_scratch = [dram(f"m_scratch{a}", (PARTS, BATCHES, 2 * HEADS, P), BF16) for a in range(2)]

        slot_full = [sem(f"slot_full{i}") for i in range(2)]
        slot_free = [sem(f"slot_free{i}") for i in range(2)]
        in_k1, in_q1, in_rope, in_v1, in_x2, in_x, in_ids, in_attn, in_ctx, in_attn2, in_masks, in_b = (
            sem(n) for n in ("in_k1", "in_q1", "in_rope", "in_v1", "in_x2", "in_x", "in_ids", "in_attn", "in_ctx", "in_attn2",
                             "in_masks", "in_b"))
        in_w = [sem(f"in_w{f}") for f in range(FT)]
        consts_ready = sem("consts_ready")
        masks_ready, v_cleared = sem("masks_ready"), sem("v_cleared")
        bias_added = sem("bias_added")
        one_ready, split_done = sem("one_ready"), sem("split_done")
        parts_stored = {s: sem("parts_stored_" + "_".join(map(str, s[1:]))) for s in PLAN if s[0] == "PROJ"}
        stacked = {s: sem("stacked_" + "_".join(map(str, s[1:]))) for s in PLAN if s[0] == "PROJ"}
        max_stored = sem("max_stored")
        max_stacked = {s: sem("max_stacked_" + "_".join(map(str, s[1:]))) for s in PLAN if s[0] == "MAXT"}
        pv_done, evac_done, turn_done, y_ready = (
            sem(n) for n in ("pv_done", "evac_done", "turn_done", "y_ready"))
        tanh_ready = sem("tanh_ready")
        bank_read_act, bank_read_dve = sem("bank_read_act"), sem("bank_read_dve")
        z_ready, var_ready, rstd_ready, norm_ready, xn_ready, x2_ready = (
            sem(n) for n in ("z_ready", "var_ready", "rstd_ready", "norm_ready", "xn_ready", "x2_ready"))
        high_done, low_done, x1_high, hidden_ready, mod_ready = (
            sem(n) for n in ("high_done", "low_done", "x1_high", "hidden_ready", "mod_ready"))
        b_ready, pair_done = sem("b_ready"), sem("pair_done")
        silu_ready, masked_ready, down_done = (sem(n) for n in ("silu_ready", "masked_ready", "down_done"))
        out_stored = sem("out_stored")
        pool_chain, dve_chain = sem("pool_chain"), sem("dve_chain")

        def slot_of(step):
            return slots[RING_AT[step][0]]

        def filled(eng, step):
            slot, value, _ = RING_AT[step]
            eng.wait_ge(slot_full[slot], value)

        def release(ins, step):
            ins.then_inc(slot_free[RING_AT[step][0]], 1)

        def released(eng, step, by=None):
            slot, _, before = RING_AT[step]
            eng.wait_ge(slot_free[slot], before + (by or RING[step[0]]))

        def chained(eng, semaphore):
            count = [0]

            def link(ins):
                count[0] += 1
                ins.then_inc(semaphore, 1)
                eng.wait_ge(semaphore, count[0])
            return link

        def split_parts(step):
            _, what, i = step
            if what == "ctx":
                return tuple(t[:, KT * i:KT * (i + 1), :] for t in (ctx_sb, ctx_h, ctx_l))
            if what == "w":
                return w_raw[:, i, :], w_h[i], w_l[:, i, :]
            return tuple(t[:, :, cols_of(i)] for t in (xhT, xh_h, xh_l))

        def hidden_parts(what, n):
            pair = (hidden_h, hidden_l) if what == "moe" else (ffn_hidden_h, ffn_hidden_l)
            return pair[0][n % 2], pair[1][n % 2]

        def norm_tiles(kind, i):
            return range(HT * i, HT * i + HT) if kind == "ln2" else range(2 * i, 2 * i + 2)

        def cols_of(u):
            return slice(HALF * u, HALF * (u + 1))

        block = ctx.enter_context(nc.Block())

        @block.sync
        def _(sp):
            sp.dma_start(wk1_sb[:], wk1).then_inc(in_k1, DMA_DONE)
            sp.dma_start(xT[:, :, 0:HALF], x_feat[:, :, 0:HALF]).then_inc(in_k1, DMA_DONE)
            sp.dma_start(wq1_sb[:], wq1).then_inc(in_q1, DMA_DONE)

            def store_parts(step):
                n = NTH[step]
                sp.wait_ge(split_done, n)
                sp.dma_start(scratch[step].rearrange("t p n -> p t n"), parts[0:rows_of(step), n % 2]) \
                    .then_inc(parts_stored[step], DMA_DONE)

            def stack(step):
                _, a, u, w, m = step
                sp.wait_ge(parts_stored[step], DMA_DONE)
                if a == 1:
                    filled(sp, ("ST", 0, BATCHES - 1, GROUPS - 1))
                heads = rows_of(step) // HD
                dst = (qs if w == "q" else ks)[:, u, P // HD * m:P // HD * m + heads, :].rearrange("p h n -> p (h n)")
                src = scratch[step].rearrange("t (d h) n -> (t d) (h n)", h=heads)
                row = 0
                for run in RUNS:
                    first = 0 if w == "q" else PARTS - run
                    sp.dma_start(dst[row:row + HD * run], src[HD * first:HD * (first + run)]) \
                        .then_inc(stacked[step], DMA_DONE)
                    row += HD * run

            def stack_maxima(step):
                _, a, b = step
                n = NTH[step]
                released(sp, step)
                sp.dma_start(m_scratch[a][:, b].rearrange("t r n -> r t n"), max_parts[:, n % 2]) \
                    .then_inc(max_stored, DMA_DONE)
                sp.wait_ge(max_stored, DMA_DONE * n)
                for qt in range(2):
                    c = SEQ * (b % 2) + P * qt
                    sp.dma_start(qs[MAX_ROW:MAX_ROW + PARTS, b // 2, :, c:c + P],
                                 m_scratch[a][:, b, HEADS * qt:HEADS * (qt + 1), :]) \
                        .then_inc(max_stacked[step], DMA_DONE)

            for step in PLAN:
                if step[0] == "PROJ":
                    store_parts(step)
                    if step[3] == "q":
                        if step[:3] + ("k", step[4]) in NTH:
                            stack(step[:3] + ("k", step[4]))
                        stack(step)
                if step == ("ST", 0, 1, 0):
                    sp.dma_start(ctx_sb[:], ctx_t).then_inc(in_ctx, DMA_DONE)
                    for dst, src in ((ln1_sb, ln1), (ln2_sb, ln2), (wq2_sb, wq2), (wk2_sb, wk2), (wv2_sb, wv2)):
                        sp.dma_start(dst[:], src).then_inc(in_attn2, DMA_DONE)
                if step[0] == "MAXT":
                    stack_maxima(step)
                if step[0] == "ST" and step[1] == 1 and 6 <= GROUPS * step[2] + step[3] < 6 + FT:
                    f = GROUPS * step[2] + step[3] - 6
                    if f == 0:
                        sp.wait_ge(down_done, NTH["DOWN", "moe", 1, EXPERTS - 1])
                        for i in range(COPIES):
                            sp.dma_start(b_raw[RANK * i:RANK * (i + 1), :], b_in).then_inc(in_b, DMA_DONE)
                    sp.dma_start(w_raw[:, f, :], w_ffn[:, f, :]).then_inc(in_w[f], DMA_DONE)
                if step[0] == "OUT":
                    pair = step[2]
                    sp.wait_ge(norm_ready, NTH["NORM", "ln3", pair] - HALVES)
                    sp.dma_start(out[:, 2 * pair:2 * pair + 2, :], X[:, 2 * pair:2 * pair + 2, :]) \
                        .then_inc(out_stored, DMA_DONE)
            sp.wait_ge(out_stored, DMA_DONE * TILES // 2)

        @block.gpsimd
        def _(pool):
            link = chained(pool, pool_chain)
            link(pool.memset(ident[:], 0.0))
            link(pool.memset(ident16[:], 0.0))
            link(pool.memset(causal_q[:], 0.0))
            link(pool.memset(causal_k[:], 0.0))
            for m in (ident, ident16):
                link(pool.affine_select(out=m[:], in_=m[:], compare_op=ALU.not_equal, fill=1.0, base=0,
                                        pattern=[[-1, P]], channel_multiplier=1))
            for lower in range(0, P, BLOCK):
                rows = slice(lower, lower + BLOCK)
                for mask, sign in ((causal_q, 1), (causal_k, -1)):
                    link(pool.affine_select(out=mask[rows], in_=mask[rows], compare_op=ALU.is_ge, fill=MASKED,
                                            base=0, pattern=[[0, GROUP], [-sign, BLOCK]],
                                            channel_multiplier=sign))
            pool.memset(minus_half[:], -0.5).then_inc(consts_ready, 1)
            pool.wait_ge(consts_ready, 1)
            link(pool.memset(v[:], 0.0))
            pool.memset(v[:, :, HD:HD + 1], 1.0).then_inc(v_cleared, 1)
            pool.wait_ge(v_cleared, 1)

            def expert_masks():
                pool.wait_ge(in_ids, DMA_DONE)
                at_least = masks[:, EXPERTS - 1, :]
                for e in range(EXPERTS - 1):
                    lo, hi = float(TOKENS_PER_EXPERT * e), float(TOKENS_PER_EXPERT * (e + 1))
                    link(pool.tensor_scalar(masks[:, e, :], ids[:], hi, None, ALU.is_lt))
                    if e:
                        link(pool.tensor_scalar(at_least, ids[:], lo, None, ALU.is_ge))
                        link(pool.tensor_tensor(masks[:, e, :], masks[:, e, :], at_least, ALU.mult))
                pool.tensor_scalar(at_least, ids[:], float(TOKENS_PER_EXPERT * (EXPERTS - 1)), None, ALU.is_ge) \
                    .then_inc(masks_ready, 1)

            for step in PLAN:
                kind = step[0]
                if step == ("V", 0, 1):
                    expert_masks()
                    pool.wait_ge(in_x, 2 * DMA_DONE)
                    for t in range(TILES):
                        ins = pool.tensor_tensor(X[:, t, :], X[:, t, :], bo1_sb[:], ALU.add)
                    ins.then_inc(bias_added, 1)
                if kind == "RSTD":
                    tiles = norm_tiles(*step[1:])
                    s = slice(tiles[0], tiles[-1] + 1)
                    pool.wait_ge(var_ready, NTH[step])
                    ins = pool.tensor_tensor(rstd[:, s], shifted[:, s], minus_half[:, s], ALU.pow)
                    if step[1] == "ln2":
                        link(ins)
                        r = rms[:, s]
                        link(pool.tensor_tensor(r, rstd[:, s], rstd[:, s], ALU.mult))
                        link(pool.tensor_tensor(r, r, moments[:, s, 1], ALU.mult))
                        link(pool.tensor_scalar(r, r, RMS_EPS, None, ALU.add))
                        link(pool.tensor_tensor(r, r, minus_half[:, s], ALU.pow))
                        ins = pool.tensor_tensor(r, r, rstd[:, s], ALU.mult)
                    ins.then_inc(rstd_ready, 1)
                if kind == "RESIDUAL":
                    pool.wait_ge(xn_ready, step[1] + 1)
                    for t in norm_tiles("ln2", step[1]):
                        ins = pool.tensor_scalar(X[:, t, :], X[:, t, :], moments[:, t, 0:1], rstd[:, t:t + 1],
                                                 ALU.subtract, ALU.mult)
                    ins.then_inc(x2_ready, 1)
                if kind == "HID" and step[1] == "moe":
                    _, _, u, e = step
                    n = NTH[step]
                    pool.wait_ge(silu_ready, n)
                    pool.wait_ge(masks_ready, 1)
                    s = silu[:, n % 2, :].rearrange("p (f n) -> p f n", f=2)
                    for f in range(2):
                        pool.tensor_tensor(s[:, f, :], s[:, f, :], masks[:, e, cols_of(u)], ALU.mult) \
                            .then_inc(masked_ready, 1)

        @block.scalar
        def _(act):
            act.dma_start(rope[:], rope_in).then_inc(in_rope, DMA_DONE)
            act.dma_start(bk1_sb[:], bk1).then_inc(in_rope, DMA_DONE)
            act.dma_start(bq1_sb[:], bq1).then_inc(in_rope, DMA_DONE)
            act.dma_start(wv1_sb[:], wv1).then_inc(in_v1, DMA_DONE)
            act.dma_start(bv1_sb[:], bv1.partition_broadcast(P)).then_inc(in_v1, DMA_DONE)
            act.dma_start(xT[:, :, HALF:TOKENS], x_feat[:, :, HALF:TOKENS]).then_inc(in_x2, DMA_DONE)
            words = "p u h (c n) -> p (u h c) n"
            rows, per_seq = slice(STACK, MAX_ROW), [HALVES * HEADS * HALF // SEQ, SEQ // 2]
            act.dma_start(qs[rows].bitcast(F32).rearrange(words, n=SEQ // 2),
                          mask_rows[0:MASK_ROWS].unsqueeze(1).broadcast_to([MASK_ROWS, *per_seq])) \
                .then_inc(in_masks, DMA_DONE)
            act.dma_start(ks[STACK:MAX_ROW + PARTS].bitcast(F32).rearrange(words, n=SEQ // 2),
                          mask_rows[MASK_ROWS:].unsqueeze(1).broadcast_to([MASK_ROWS + PARTS, *per_seq])) \
                .then_inc(in_masks, DMA_DONE)
            act.dma_start(ids[:], token_ids.partition_broadcast(P)) \
                .then_inc(in_ids, DMA_DONE)
            for dst, src in ((wo1_sb, wo1), (wo2_sb, wo2), (a_sb, a_in)):
                act.dma_start(dst[:], src).then_inc(in_attn, DMA_DONE)
            act.dma_start(X[:], x_tok).then_inc(in_x, DMA_DONE)
            act.dma_start(bo1_sb[:], bo1.partition_broadcast(P)).then_inc(in_x, DMA_DONE)

            for step in PLAN:
                kind = step[0]
                if kind == "ST":
                    n = NTH[step]
                    filled(act, step)
                    if n > BUFFERS:
                        act.wait_ge(pv_done, n - BUFFERS)
                    for banks in (slice(0, 2 * HALF), slice(2 * HALF, 3 * HALF)):
                        release(act.activation(probs[:, (n - 1) % BUFFERS, banks], slot_of(step)[:, banks],
                                               ACT.Exp, scale=SM_SCALE), step)

                if kind == "PROJ" and step[1] == 1:
                    n = NTH[step]
                    filled(act, step)
                    act.wait_ge(parts_stored[step_at("PROJ", n - 2)], DMA_DONE)
                    act.activation(parts[:, n % 2, 0 if step[3] == "q" else PARTS - 1, :], slot_of(step)[:, 0:HALF],
                                   ACT.Copy).then_inc(one_ready, 1)
                if kind == "V" and step[1] == 1:
                    u = step[2]
                    last = ("PV", 1, 1, GROUPS - 1) if u else ("PV", 0, BATCHES - 1, GROUPS - 1)
                    filled(act, step)
                    act.wait_ge(v_cleared, 1)
                    act.wait_ge(pv_done, NTH[last])
                    release(act.activation(v[:, :, 0:HD], slot_of(step)[:, 0:HT * D] \
                                           .rearrange("p (n d) -> p n d", d=HD), ACT.Copy), step)
                if kind == "EVAC":
                    n = NTH[step]
                    act.wait_ge(pv_done, NTH["PV", step[1], step[2], 2 * step[3] + 1])
                    if n > 1:
                        act.wait_ge(turn_done, n - 1)
                    act.activation(o_sb[:], attn_out[:], ACT.Copy).then_inc(evac_done, 1)
                if kind == "YT":
                    n = NTH[step]
                    filled(act, step)
                    if n > 2:
                        a, b = divmod(n - 3, BATCHES)
                        filled(act, ("MOD" if a else "WO", a, b))
                    release(act.activation(yT[:, n % 2].rearrange("p k n -> p (k n)"), slot_of(step)[:, 0:HALF],
                                           ACT.Copy), step)
                if kind == "TR":
                    _, what, u = step
                    filled(act, step)
                    src = slot_of(step)
                    if what == "x1":
                        for k in range(KT):
                            ins = act.activation(x1_h[u][:, k, :], src[:, HALF * k:HALF * (k + 1)], ACT.Copy)
                            if k == 0:
                                ins.then_inc(x1_high, 1)
                    else:
                        act.wait_ge(in_attn2, 5 * DMA_DONE)
                        for k in (1, 0):
                            if k == 0:
                                act.wait_ge(bank_read_dve, u + 1)
                            ins = act.activation(xmT[:, k, cols_of(u)], src[:, HALF * k:HALF * (k + 1)], ACT.Copy,
                                                 scale=ln1_sb[:, k:k + 1])
                            if k == 1:
                                ins.then_inc(bank_read_act, 1)
                    release(ins, step)
                if kind == "SPLIT":
                    if step[1] == "ctx":
                        act.wait_ge(in_ctx, DMA_DONE)
                    elif step[1] == "w":
                        act.wait_ge(in_w[step[2]], DMA_DONE)
                        if step[2] < EARLY:
                            filled(act, ("V", 1, 1))
                        else:
                            filled(act, ("ST", 1, BATCHES - 1, GROUPS - 1))
                    src, high, _ = split_parts(step)
                    act.activation(high, src, ACT.Copy).then_inc(high_done, 1)
                if kind == "HID":
                    n = NTH[step]
                    width = 2 * HALF if step[1] == "moe" else HALF
                    filled(act, step)
                    if n > 2:
                        act.wait_ge(hidden_ready, n - 2)
                    act.activation(silu[:, n % 2, 0:width], slot_of(step)[:, 0:width], ACT.Silu) \
                        .then_inc(silu_ready, 1)
                if kind == "MOD":
                    filled(act, step)
                    if NTH[step] > 1:
                        act.wait_ge(mod_ready, NTH[step] - 1)
                    act.activation(tanh[:], slot_of(step)[0:COPIES * RANK, 0:SEQ], ACT.Tanh).then_inc(tanh_ready, 1)

        @block.vector
        def _(dve):
            link = chained(dve, dve_chain)
            def split(step):
                _, a, u, w, m = step
                n = NTH[step]
                rows = rows_of(step)
                src, rest, part = slot_of(step)[0:rows, 0:HALF], full[0:rows, n % 2, :], parts[0:rows, n % 2]
                filled(dve, step)
                if n == 1:
                    dve.wait_ge(in_rope, 3 * DMA_DONE)
                if a == 0:
                    bias = bq1_sb[:, m:m + 1] if w == "q" else bk1_sb[:, 0:1]
                    for j in range(HALF // SEQ):
                        c = slice(SEQ * j, SEQ * (j + 1))
                        ins = dve.scalar_tensor_tensor(out=rest[:, c], in0=src[:, c], scalar=bias,
                                                       in1=rope[0:rows, w == "k", :], op0=ALU.add, op1=ALU.mult)
                    release(ins, step)
                    released(dve, step)
                    src = rest
                if n > 2:
                    dve.wait_ge(parts_stored[step_at("PROJ", n - 2)], DMA_DONE)
                one, two, three = (part[:, i, :] for i in (range(PARTS) if w == "q" else reversed(range(PARTS))))
                if a == 0:
                    link(dve.tensor_copy(one, src))
                else:
                    dve.wait_ge(one_ready, n - step_count("PROJ", 0))
                ins = dve.tensor_tensor(rest, src, one, ALU.subtract)
                if a == 1:
                    release(ins, step)
                    released(dve, step)
                else:
                    link(ins)
                link(dve.tensor_copy(two, rest))
                dve.tensor_tensor(three, rest, two, ALU.subtract).then_inc(split_done, 1)

            def moments_of(step, tiles, eps, scale=None):
                for t in tiles:
                    ins = dve.bn_stats(stats[:, t, :], X[:, t, :])
                link(ins)
                for t in tiles:
                    ins = dve.bn_aggr(moments[:, t, :], stats[:, t, :])
                link(ins)
                s = slice(tiles[0], tiles[-1] + 1)
                dve.tensor_scalar(shifted[:, s], moments[:, s, 1], eps, None, ALU.add).then_inc(var_ready, 1)

            for step in PLAN:
                kind = step[0]
                if kind == "PROJ":
                    split(step)
                if kind == "V" and step[1] == 0:
                    u = step[2]
                    filled(dve, step)
                    dve.wait_ge(v_cleared, 1)
                    dve.wait_ge(in_v1, 2 * DMA_DONE)
                    four = "p (t h d) -> p t h d"
                    release(dve.tensor_tensor(
                        v1[:, HT * u:HT * (u + 1), :, 0:HD],
                        slot_of(step)[:, 0:HT * KV_HEADS * HD].rearrange(four, t=HT, d=HD),
                        bv1_sb[:].rearrange("p (t h d) -> p t h d", t=1, d=HD).broadcast_to([P, HT, KV_HEADS, HD]),
                        ALU.add), step)
                if kind == "S":
                    _, a, b, g = step
                    n = NTH["MAXT", a, b]
                    filled(dve, step)
                    if g == 0 and n > 2:
                        filled(dve, step_at("MAXT", n - 2))
                    src = slot_of(step)
                    h = GROUP * g
                    ins = dve.tensor_reduce(neg_max[:, n % 2, HEADS + h:HEADS + h + GROUP],
                                            src[:, 0:2 * HALF].rearrange("p (c h k) -> p h c k", c=2, h=GROUP),
                                            AXY, ALU.max, negate=True)
                    release(ins, step)
                    ins = dve.tensor_reduce(neg_max[:, n % 2, h:h + GROUP],
                                            src[:, 2 * HALF:3 * HALF].rearrange("p (h k) -> p h k", h=GROUP),
                                            AX, ALU.max, negate=True)
                    release(ins, step)
                if kind == "MAXT":
                    n = NTH[step]
                    filled(dve, step)
                    if n > 2:
                        dve.wait_ge(max_stored, DMA_DONE * (n - 2))
                    src = slot_of(step)[0:2 * HEADS, 0:P]
                    m = max_parts[:, n % 2]
                    link(dve.tensor_copy(m[:, 0, :], src))
                    link(dve.tensor_tensor(max_rest[:], src, m[:, 0, :], ALU.subtract))
                    link(dve.tensor_copy(m[:, 1, :], max_rest[:]))
                    release(dve.tensor_tensor(m[:, 2, :], max_rest[:], m[:, 1, :], ALU.subtract), step)
                if kind == "TURN":
                    _, a, b, pair = step
                    n = NTH[step]
                    dve.wait_ge(turn_done, n)
                    if pair == 0 and (a, b) != (0, 0):
                        filled(dve, ("YT", a, b - 1) if b else ("YT", 0, BATCHES - 1))
                    src = turned_ps[:].rearrange("p (q h w) -> p q h w", q=2, w=VW)
                    link(dve.reciprocal(inv_sum[:], src[:, :, :, HD]))
                    w = 2 * GROUP * HD
                    dve.tensor_tensor(y[:, :, w * pair:w * (pair + 1)].rearrange("p q (h d) -> p q h d", d=HD),
                                      src[:, :, :, 0:HD],
                                      inv_sum[:].unsqueeze(3).broadcast_to([P, 2, 8, HD]), ALU.mult) \
                        .then_inc(y_ready, 1)
                if kind == "WO":
                    _, a, b = step
                    filled(dve, step)
                    dve.wait_ge(bias_added, 1)
                    release(dve.tensor_tensor(X[:, 2 * b:2 * b + 2, :], X[:, 2 * b:2 * b + 2, :],
                                              slot_of(step)[:, 0:2 * D].rearrange("p (t n) -> p t n", t=2),
                                              ALU.add), step)
                    released(dve, step)
                if kind == "RSTD":
                    _, what, i = step
                    tiles = norm_tiles(what, i)
                    if what == "ln1":
                        moments_of(step, tiles, LN_EPS)
                    else:
                        if what == "ln2":
                            dve.wait_ge(down_done, NTH["DOWN", "moe", i, EXPERTS - 1])
                        else:
                            if i % 2 == 0:
                                dve.wait_ge(pair_done, i // 2 + 1)
                            else:
                                dve.wait_ge(down_done, NTH["DOWN", "ffn", i // 2, FT - 1])
                            dve.wait_ge(x2_ready, i // 2 + 1)
                        for t in tiles[::2]:
                            xs = X[:, t:t + 2, :].rearrange("p t n -> p (t n)")
                            ins = dve.scalar_tensor_tensor(out=xs, in0=xs, scalar=1.0 if what == "ln2" else 2.0,
                                                           in1=accs[t // 2 % 2][:], op0=ALU.mult, op1=ALU.add)
                        ins.then_inc(z_ready, 1)
                        dve.wait_ge(z_ready, i + 1 + (HALVES if what == "ln3" else 0))
                        moments_of(step, tiles, LN_EPS)
                if kind == "NORM":
                    _, what, i = step
                    dve.wait_ge(rstd_ready, NTH[step])
                    if what == "ln2":
                        if i:
                            filled(dve, ("TR", "xn", i - 1))
                        else:
                            dve.wait_ge(masks_ready, 1)
                        for j, t in enumerate(norm_tiles(what, i)):
                            ins = dve.tensor_scalar(xn[:, j, :], X[:, t, :], moments[:, t, 0:1], rms[:, t:t + 1],
                                                    ALU.subtract, ALU.mult)
                        ins.then_inc(xn_ready, 1)
                        continue
                    for t in norm_tiles(what, i):
                        ins = dve.tensor_scalar(X[:, t, :], X[:, t, :], moments[:, t, 0:1], rstd[:, t:t + 1],
                                                ALU.subtract, ALU.mult)
                    ins.then_inc(norm_ready, 1)
                if kind == "TR":
                    _, what, u = step
                    filled(dve, step)
                    src = slot_of(step)
                    if what == "x1":
                        for k in range(KT):
                            if k == 0:
                                dve.wait_ge(x1_high, u + 1)
                            else:
                                released(dve, step, 1)
                            ins = dve.tensor_tensor(x1_l[u][:, k, :], src[:, HALF * k:HALF * (k + 1)],
                                                    x1_h[u][:, k, :].bitcast(F32), ALU.subtract)
                    else:
                        dve.wait_ge(in_attn2, 5 * DMA_DONE)
                        for k in (0, 1):
                            if k == 1:
                                dve.wait_ge(bank_read_act, u + 1)
                            ins = dve.tensor_scalar(xhT[:, k, cols_of(u)], src[:, HALF * k:HALF * (k + 1)],
                                                    ln2_sb[:, k:k + 1], None, ALU.mult)
                            if k == 0:
                                ins.then_inc(bank_read_dve, 1)
                    release(ins, step)
                if kind == "MULT":
                    _, what, u, i = step
                    step, n = ("HID", what, u, i), NTH[step]
                    if n > 2:
                        dve.wait_ge(down_done, n - 2)
                    width = 2 * HALF if what == "moe" else HALF
                    h = silu[:, n % 2, 0:width]
                    if what == "moe":
                        for f in range(2):
                            dve.wait_ge(masked_ready, 2 * n - 1 + f)
                            c = slice(HALF * f, HALF * (f + 1))
                            ins = dve.tensor_tensor(h[:, c], h[:, c], slot_of(step)[:, c], ALU.mult)
                    else:
                        dve.wait_ge(silu_ready, n)
                        ins = dve.tensor_tensor(h, h, slot_of(step)[:, HALF:2 * HALF], ALU.mult)
                    release(ins, step)
                    released(dve, step)
                    high, low = hidden_parts(what, n)
                    if step == ("HID", "ffn", 0, 0):
                        filled(dve, ("ST", 1, BATCHES - 1, GROUPS - 1))
                    link(dve.tensor_copy(high[:], h))
                    dve.tensor_tensor(low[:], h, high[:].bitcast(F32), ALU.subtract) \
                        .then_inc(hidden_ready, 1)
                if kind == "SPLIT":
                    dve.wait_ge(high_done, NTH[step])
                    src, high, low = split_parts(step)
                    if step[1] == "x":
                        filled(dve, ("MOD", 1, 2 * step[2] + 1))
                    dve.tensor_tensor(low, src, high.bitcast(F32), ALU.subtract).then_inc(low_done, 1)
                if kind == "SPLIT_B":
                    dve.wait_ge(in_b, COPIES * DMA_DONE)
                    link(dve.tensor_copy(b3[:], b_raw[:]))
                    last = slice((COPIES - 1) * RANK, COPIES * RANK)
                    dve.tensor_tensor(b3[last, :], b_raw[last, :], b3[last, :].bitcast(F32), ALU.subtract) \
                        .then_inc(b_ready, 1)
                if kind == "MOD":
                    _, a, b = step
                    dve.wait_ge(tanh_ready, NTH[step])
                    release(dve.scalar_tensor_tensor(out=tanh[:], in0=tanh[:], scalar=MOD_SCALE,
                                                     in1=slot_of(step)[0:COPIES * RANK, HALF:HALF + SEQ],
                                                     op0=ALU.mult, op1=ALU.mult), step)
                    released(dve, step)
                    m = modT[:, SEQ * b:SEQ * (b + 1)]
                    link(dve.tensor_copy(m, tanh[:]))
                    dve.tensor_tensor(m[0:RANK], tanh[0:RANK, :], m[0:RANK].bitcast(F32), ALU.subtract) \
                        .then_inc(mod_ready, 1)
                if kind == "WOA":
                    filled(dve, step)
                    release(dve.tensor_copy(woa_sb[:].rearrange("p k r -> p (k r)"),
                                            slot_of(step)[:, 0:KT * COPIES * RANK]), step)

        @block.tensor
        def _(pe):
            mm = pe.matmul

            def split_mm(dst, operands, start=True, stop=True):
                passes = [(a, b) for a_h, a_l, b_h, b_l in operands for a, b in ((a_h, b_h), (a_h, b_l), (a_l, b_h))]
                for j, (a, b) in enumerate(passes):
                    ins = mm(dst, a, b, start=start and j == 0, stop=stop and j == len(passes) - 1,
                             skip_group_check=True)
                return ins

            def take(step):
                slot, _, before = RING_AT[step]
                if before:
                    pe.wait_ge(slot_free[slot], before - TAIL[step])
                return slots[slot]

            def take_bank_2(step):
                slot, _, before = RING_AT[step]
                if TAIL[step]:
                    pe.wait_ge(slot_free[slot], before)

            def give(ins, step):
                ins.then_inc(slot_full[RING_AT[step][0]], 1)

            def project(step):
                _, a, u, w, m = step
                dst = take(step)
                rows = rows_of(step)
                if a == 0:
                    pe.wait_ge(in_k1, 2 * DMA_DONE)
                    if w == "q":
                        pe.wait_ge(in_q1, DMA_DONE)
                    if u:
                        pe.wait_ge(in_x2, DMA_DONE)
                    x, weights = xT, wq1_sb if w == "q" else wk1_sb
                else:
                    released(pe, ("TR", "xn", u))
                    pe.wait_ge(in_attn2, 5 * DMA_DONE)
                    x, weights = xmT, wq2_sb if w == "q" else wk2_sb
                for k in range(KT):
                    ins = mm(dst[0:rows, 0:HALF], weights[:, k, P * m:P * m + rows], x[:, k, cols_of(u)],
                             start=k == 0, stop=k == KT - 1)
                give(ins, step)

            def values(step):
                _, a, u = step
                dst = take(step)
                x, weights, w = (xmT, wv2_sb, D) if a else (xT, wv1_sb, KV_HEADS * HD)
                if a == 0:
                    pe.wait_ge(in_v1, 2 * DMA_DONE)
                    if u:
                        pe.wait_ge(in_x2, DMA_DONE)
                for t in range(HT):
                    for k in range(KT):
                        c = HALF * u + P * t
                        ins = mm(dst[:, w * t:w * (t + 1)], x[:, k, c:c + P], weights[:, k, :],
                                 start=k == 0, stop=k == KT - 1)
                give(ins, step)

            def kv(a, h):
                return h if a else h // (HEADS // KV_HEADS)

            def scores(step):
                _, a, b, g = step
                dst = take(step)
                for w, m in (("q", g // 2), ("k", g // 2 if a else 0)):
                    pe.wait_ge(stacked["PROJ", a, b // 2, w, m], DMA_DONE * len(RUNS))
                if g == 0 and b == 0 and a == 0:
                    pe.wait_ge(consts_ready, 1)
                    pe.wait_ge(in_masks, 2 * DMA_DONE)
                u, c = b // 2, SEQ * (b % 2)
                for bank, (qt, kt) in enumerate(((1, 0), (1, 1), (0, 0))):
                    if bank == 2:
                        take_bank_2(step)
                    for j in range(GROUP):
                        h = GROUP * g + j
                        at = HALF * bank + P * j
                        ins = mm(dst[:, at:at + P], qs[0:MAX_ROW, u, h, c + P * qt:c + P * (qt + 1)],
                                 ks[0:MAX_ROW, u, kv(a, h), c + P * kt:c + P * (kt + 1)],
                                 start=j == 0, stop=bank == 0 and j == GROUP - 1, skip_group_check=True)
                give(mask_blocks(dst, (1, 2), causal_q), step)

            def mask_blocks(dst, banks, triangles):
                for bank in banks:
                    heads = dst[:, HALF * bank:HALF * (bank + 1)].rearrange("p (h n) -> p h n", h=GROUP)
                    for at in range(0, P, BLOCK):
                        s = slice(at, at + BLOCK)
                        ins = mm(heads[s, :, s], ident16[:, s], triangles[:], start=False, stop=True,
                                 skip_group_check=True, tile_position=(0, at))
                return ins

            def turn_maxima(step):
                n = NTH[step]
                dst = take(step)
                released(pe, ("S", step[1], step[2], GROUPS - 1))
                give(pe.transpose(dst[0:2 * HEADS, 0:P], neg_max[:, n % 2, :], ident[:]), step)

            def scores_turned(step):
                _, a, b, g = step
                dst = take(step)
                pe.wait_ge(max_stacked["MAXT", a, b], 2 * DMA_DONE)
                u, c, rows = b // 2, SEQ * (b % 2), MAX_ROW + PARTS
                per = 1 if a else GROUP
                for bank, (kt, qt) in enumerate(((0, 0), (0, 1), (1, 1))):
                    if bank == 2:
                        take_bank_2(step)
                    for j in range(0, GROUP, per):
                        h = GROUP * g + j
                        at = HALF * bank + P * j
                        mm(dst[:, at:at + P * per], ks[0:rows, u, kv(a, h), c + P * kt:c + P * (kt + 1)],
                           qs[0:rows, u, h:h + per, c + P * qt:c + P * (qt + 1)], start=j == 0,
                           stop=bank == 1 and j + per == GROUP, skip_group_check=True)
                give(mask_blocks(dst, (0, 2), causal_k), step)

            def weigh_values(step):
                _, a, b, g = step
                n = NTH["ST", a, b, g]
                released(pe, ("ST", a, b, g))
                if g == 0:
                    released(pe, ("V", a, b // 2))
                if g % 2 == 0:
                    done = NTH["EVAC", a, b, g // 2] - 1
                    if done:
                        pe.wait_ge(evac_done, done)
                    if (a, b, g) == (1, 0, 0):
                        pe.wait_ge(z_ready, HALVES)
                e = probs[:, (n - 1) % BUFFERS, :]
                blocks = e.rearrange("p (c h q) -> p c h q", c=3, h=GROUP)
                at = SEQ * (g % 2)
                out_cols = attn_out[:, at:at + SEQ].rearrange("p (q n) -> p q n", q=2)
                for kt in range(2):
                    for j in range(GROUP):
                        rows = slice(VW * j, VW * (j + 1))
                        vt = (v2[:, 2 * (b % 2) + kt, GROUP * g + j, :] if a else v1[:, 2 * b + kt, g, :])
                        ins = mm(out_cols[rows, 1, :] if kt else out_cols[rows], vt,
                                 blocks[:, 2, j, :] if kt else blocks[:, 0:2, j, :],
                                 start=kt == 0 and g % 2 == 0, stop=kt == 1, skip_group_check=True,
                                 tile_position=(0, VW * j))
                ins.then_inc(pv_done, 1)

            def turn_outputs(step):
                n = NTH[step]
                pe.wait_ge(evac_done, n)
                if n > 1:
                    pe.wait_ge(y_ready, n - 1)
                for qt in range(2):
                    for gg in range(2):
                        src = SEQ * gg + P * qt
                        dst = P * (2 * qt + gg)
                        ins = pe.transpose(turned_ps[:, dst:dst + P], o_sb[:, src:src + P], ident[:])
                ins.then_inc(turn_done, 1)

            def turn_y(step):
                _, a, b = step
                dst = take(step)
                pe.wait_ge(y_ready, NTH["TURN", a, b, 1])
                for k in range(KT):
                    for qt in range(2):
                        at = SEQ * k + P * qt
                        ins = pe.transpose(dst[:, at:at + P], y[:, qt, P * k:P * (k + 1)], ident[:])
                give(ins, step)

            def output_product(step):
                _, a, b = step
                dst = take(step)
                n = NTH["YT", a, b]
                released(pe, ("YT", a, b))
                pe.wait_ge(in_attn, 3 * DMA_DONE)
                for qt in range(2):
                    for k in range(KT):
                        ins = mm(dst[:, D * qt:D * (qt + 1)], yT[:, n % 2, k, P * qt:P * (qt + 1)], wo1_sb[:, k, :],
                                 start=k == 0, stop=k == KT - 1)
                give(ins, step)

            def modulation(step):
                _, a, b = step
                dst = take(step)
                n = NTH["YT", a, b]
                for k in range(KT):
                    mm(dst[0:COPIES * RANK, HALF:HALF + SEQ], a_sb[:, k, :], xhT[:, k, SEQ * b:SEQ * (b + 1)],
                       start=k == 0, stop=k == KT - 1)
                released(pe, ("YT", a, b))
                released(pe, ("WOA",))
                for k in range(KT):
                    ins = mm(dst[0:COPIES * RANK, 0:SEQ], woa_sb[:, k, :], yT[:, n % 2, k, :],
                             start=k == 0, stop=k == KT - 1)
                give(ins, step)

            def fold(step):
                dst = take(step)
                pe.wait_ge(in_attn, 3 * DMA_DONE)
                for m in range(KT):
                    for k in range(KT):
                        ins = mm(dst[:, COPIES * RANK * m:COPIES * RANK * (m + 1)], wo2_sb[:, k, P * m:P * (m + 1)], a_sb[:, k, :],
                                 start=k == 0, stop=k == KT - 1)
                give(ins, step)

            def turn_tokens(step):
                _, what, u = step
                dst = take(step)
                if what == "x1":
                    pe.wait_ge(norm_ready, NTH["NORM", "ln1", 2 * u + 1])
                else:
                    pe.wait_ge(xn_ready, u + 1)
                for k in range(KT):
                    for t in range(HT):
                        src = (X[:, HT * u + t] if what == "x1" else xn[:, t])[:, P * k:P * (k + 1)]
                        at = HALF * k + P * t
                        ins = pe.transpose(dst[:, at:at + P], src, ident[:])
                give(ins, step)

            def hidden_products(step):
                _, what, u, i = step
                dst = take(step)
                if what == "moe":
                    if i == 0:
                        released(pe, ("TR", "x1", u))
                    pe.wait_ge(low_done, NTH["SPLIT", "ctx", i])
                    for f in range(2):
                        ins = split_mm(dst[:, HALF * f:HALF * (f + 1)],
                                       [(ctx_h[:, KT * i + k, P * f:P * (f + 1)], ctx_l[:, KT * i + k, P * f:P * (f + 1)],
                                         x1_h[u][:, k, :], x1_l[u][:, k, :]) for k in range(KT)])
                else:
                    if i == 0:
                        pe.wait_ge(mod_ready, NTH["MOD", 1, 2 * u + 1])
                        pe.wait_ge(b_ready, 1)
                    if u == 0:
                        pe.wait_ge(low_done, NTH["SPLIT", "w", i])
                    elif i == 0:
                        pe.wait_ge(low_done, NTH["SPLIT", "x", 1])
                    c = cols_of(u)
                    for half, side in enumerate((0, KT * P)):
                        if half == 0:
                            mm(dst[:, 0:HALF], b3[:, P * i:P * (i + 1)], modT[:, c], start=True, stop=False,
                               skip_group_check=True)
                        ins = split_mm(dst[:, HALF * half:HALF * (half + 1)],
                                       [(w_h[i][:, side + P * k:side + P * (k + 1)],
                                         w_l[:, i, side + P * k:side + P * (k + 1)],
                                         xh_h[:, k, c], xh_l[:, k, c]) for k in range(KT)], start=half == 1)
                give(ins, step)

            def down_product(step):
                _, what, u, i = step
                n = NTH["HID", what, u, i]
                pe.wait_ge(hidden_ready, n)
                if i == 0:
                    if what == "moe":
                        if u == 0:
                            pe.wait_ge(evac_done, NTH["EVAC", 0, BATCHES - 1, 1])
                            pe.wait_ge(y_ready, NTH["TURN", 0, BATCHES - 1, 1])
                        else:
                            pe.wait_ge(z_ready, 1)
                    elif u == 0:
                        pe.wait_ge(evac_done, NTH["EVAC", 1, BATCHES - 1, 1])
                        pe.wait_ge(y_ready, NTH["TURN", 1, BATCHES - 1, 1])
                    else:
                        pe.wait_ge(z_ready, HALVES + 2)
                ktiles, last = (2, EXPERTS - 1) if what == "moe" else (1, FT - 1)
                high, low = hidden_parts(what, n)
                for k in range(ktiles):
                    for t in range(HT):
                        at = HALF * k + P * t
                        if what == "moe":
                            rhs = ctx_h[:, ktiles * i + k, :], ctx_l[:, ktiles * i + k, :]
                        else:
                            rhs = w_h[i][:, 2 * D:WIDE], w_l[:, i, 2 * D:WIDE]
                        ins = split_mm(accs[t // 2][:, D * (t % 2):D * (t % 2 + 1)],
                                       [(high[:, at:at + P], low[:, at:at + P], *rhs)],
                                       start=i == 0 and k == 0 and t % 2 == 0, stop=i == last and k == ktiles - 1)
                        if what == "ffn" and i == last and t == 1:
                            ins.then_inc(pair_done, 1)
                ins.then_inc(down_done, 1)

            parts_of = {"PROJ": project, "V": values, "S": scores, "MAXT": turn_maxima, "ST": scores_turned,
                        "PV": weigh_values, "TURN": turn_outputs, "YT": turn_y, "WO": output_product,
                        "MOD": modulation, "WOA": fold, "TR": turn_tokens, "HID": hidden_products,
                        "DOWN": down_product}
            for step in PLAN:
                if step[0] in parts_of:
                    parts_of[step[0]](step)


def rope_tables():
    inv = np.float32(10000.0) ** (np.float32(-2.0) * np.arange(HD // 2, dtype=np.float32) / np.float32(HD))
    theta = np.arange(SEQ, dtype=np.float32)[:, None] * inv[None, :].astype(np.float32)
    table = (np.cos(theta) + np.sin(theta)).T.astype(np.float32)
    tables = np.zeros((P, 2, SEQ), np.float32)
    tables[:, 0] = np.repeat(np.tile(table, (2, 1)), P // HD, axis=0)
    tables[0:KV_HEADS * HD, 1] = np.repeat(np.tile(table, (2, 1)), KV_HEADS, axis=0)
    return tables


def stack_mask_rows():
    block = np.arange(SEQ) // BLOCK
    of_row = np.arange(MASK_ROWS)[:, None]
    rows = np.concatenate([block == of_row, MASKED * (block > of_row), np.ones((PARTS, SEQ))]).astype(np.float32)
    return (np.ascontiguousarray(rows).view(np.uint32) >> 16).astype(np.uint16).view(np.float32)


def kernel(**inputs):
    import concourse.bacc as bacc
    from concourse.bass_utils import run_bass_kernel_spmd

    g = {n: np.asarray(a) for n, a in inputs.items()}

    def by_place(a):
        heads = min(P, a.shape[0]) // HD
        return a.reshape(-1, heads, HD, *a.shape[1:]).swapaxes(1, 2).reshape(a.shape)

    def weight(name, order=lambda a: a):
        w = order(g[name])
        return w.T.reshape(-1, P, w.shape[0]).transpose(1, 0, 2)

    def columns(a):
        return a.reshape(-1, P).T

    def by_hidden_tile(name):
        return weight(name).reshape(P, KT, FT, P).transpose(0, 2, 1, 3).reshape(P, FT, KT * P)

    x = g["x"].reshape(TOKENS, D)
    arrays = {
        "x_tok": x.reshape(TILES, P, D).transpose(1, 0, 2),
        "x_feat": x.T.reshape(KT, P, TOKENS).transpose(1, 0, 2),
        "token_ids": g["itok_BxS_13_99985"].reshape(TOKENS),
        "ctx_t": g["ctx_2048"].transpose(0, 2, 1).reshape(EXPERTS * KT, P, EF).transpose(1, 0, 2),
        "wq1": weight("L0_attn_Wq", by_place), "bq1": columns(by_place(g["L0_attn_bq"])),
        "wk1": weight("L0_attn_Wk", by_place), "bk1": by_place(g["L0_attn_bk"]).reshape(-1, 1),
        "wv1": weight("L0_attn_Wv"), "bv1": g["L0_attn_bv"],
        "wo1": weight("L0_attn_Wo"), "bo1": g["L0_attn_bo"],
        "ln1": columns(g["L0_ffn_ln1_w"]), "ln2": columns(g["L0_ffn_ln2_w"]),
        "wq2": weight("L0_ffn_Wq", by_place), "wk2": weight("L0_ffn_Wk", by_place), "wv2": weight("L0_ffn_Wv"),
        "wo2": g["L0_ffn_Wo"].reshape(KT, P, D).transpose(1, 0, 2),
        "a_in": np.tile(g["L0_ffn_A"].reshape(KT, P, RANK).transpose(1, 0, 2), (1, 1, COPIES)),
        "b_in": g["L0_ffn_B"],
        "w_ffn": np.concatenate([by_hidden_tile("L0_ffn_W_in_base"), by_hidden_tile("L0_ffn_W_up_base"),
                                 weight("L0_ffn_W_down")], axis=2),
        "rope_in": rope_tables(), "mask_rows": stack_mask_rows(),
    }
    nc = bacc.Bacc("TRN2", target_bir_lowering=False, num_devices=1)
    args = []
    for name, a in arrays.items():
        a = arrays[name] = np.ascontiguousarray(a)
        args.append(nc.dram_tensor(name, a.shape, mybir.dt.from_np(a.dtype), kind="ExternalInput").ap())
    args.append(nc.dram_tensor("out", (P, TILES, D), F32, kind="ExternalOutput").ap())
    decoder_layer(nc, *args)
    got = run_bass_kernel_spmd(nc, [arrays], core_ids=[0]).results[0]["out"]
    return np.ascontiguousarray(got.transpose(1, 0, 2)).reshape(BATCHES, SEQ, D)
```
